# Optimizing a Trainium2 kernel written in Bass

```python
import numpy as np
import jax
import jax.numpy as jnp

def _softmax(x, axis=-1):
    return jax.nn.softmax(x, axis=axis)

def _gelu(x):
    return jax.nn.gelu(x, approximate=True)

def _silu(x):
    return jax.nn.silu(x)

def _sigmoid(x):
    return jax.nn.sigmoid(x)

def _layernorm(x, axis=-1, eps=1e-05):
    m = jnp.mean(x, axis=axis, keepdims=True)
    v = jnp.var(x, axis=axis, keepdims=True)
    return (x - m) / jnp.sqrt(v + eps)

def _scatter_add(tgt, idx, src, axis=0):
    return tgt.at[idx].add(src)

def _segment_sum(src, seg, n):
    return jax.ops.segment_sum(src, seg, n)
kernel_name = 'mk_decoder_postln_d1_seqx_r2_5c42e1'

def setup_inputs(seed: int=0):
    np.random.seed(seed)
    _w = jnp.asarray

    def _rec_inputs():
        import jax
        import jax.numpy as jnp
        _rk = jax.random.key(seed)
        x = -0.0002928 + 1 * jax.random.normal(jax.random.fold_in(_rk, 1), (32, 256, 512), jnp.float32)
        _lenS = 256 - jax.random.randint(jax.random.fold_in(_rk, 7), (32,), 0, max(1, 256 // 4) + 1, jnp.int32)
        _lenS2 = 256 - jax.random.randint(jax.random.fold_in(_rk, 8), (32,), 0, max(1, 256 // 4) + 1, jnp.int32)
        _ctx_1024P = jax.random.normal(jax.random.fold_in(_rk, 11), (32, 16, 512), jnp.float32)
        _ctx_1024c = jax.random.dirichlet(jax.random.fold_in(_rk, 511), 0.3 * jnp.ones((16,), jnp.float32), (32, 256))
        _ctx_1024t = jnp.einsum('bsk,bkd->bsd', _ctx_1024c, _ctx_1024P)
        _ctx_1024t = _ctx_1024t * jax.lax.rsqrt(jnp.mean(jnp.square(_ctx_1024t)) + 1e-12) * 0.953939
        ctx_1024 = -1.39393e-06 + 0.999914 * (_ctx_1024t + 0.3 * jax.random.normal(jax.random.fold_in(_rk, 611), (32, 256, 512), jnp.float32))
        return (x, ctx_1024)
    x, ctx_1024 = _rec_inputs()

    def _L0_attn_setup():
        import jax, jax.numpy as jnp
        import numpy as np
        B, T, D, H = (4, 1024, 512, 16)
        HEAD_DIM = D // H
        LOCAL_WINDOW = 256

        def _rotate_half(t):
            t1, t2 = jnp.split(t, 2, axis=-1)
            return jnp.concatenate([-t2, t1], axis=-1)

        def _apply_rope(q, k):
            Tq, d = (q.shape[2], q.shape[3])
            half = d // 2
            theta = 1.0 / 10000.0 ** (jnp.arange(half, dtype=jnp.float32) / half)
            pos = jnp.arange(Tq, dtype=jnp.float32)
            freqs = pos[:, None] * theta[None, :]
            freqs = jnp.concatenate([freqs, freqs], axis=-1)
            cos = jnp.cos(freqs)[None, None]
            sin = jnp.sin(freqs)[None, None]
            q = q * cos + _rotate_half(q) * sin
            k = k * cos + _rotate_half(k) * sin
            return (q, k)
        key = jax.random.key(seed)
        k1, k2, k3 = jax.random.split(key, 3)
        x = jax.random.normal(k1, (B, T, D), dtype=jnp.float32)
        Wqkv = jax.random.normal(k2, (D, 3 * D), dtype=jnp.float32) * 0.02
        Wout = jax.random.normal(k3, (D, D), dtype=jnp.float32) * 0.02
        return {'x': x, 'Wqkv': Wqkv, 'Wout': Wout}
    _L0_attn_all = _L0_attn_setup()
    _L0_attn_in = {k: v for k, v in _L0_attn_all.items() if k in ('Wqkv', 'Wout')}
    del _L0_attn_all

    def _L0_xattn_setup():
        import jax, jax.numpy as jnp
        import numpy as np
        B, S, E, NH = (2, 1024, 512, 4)
        HD = E // NH

        def _mlstm_head(q, k, v, ig, fg, eps=1e-06):
            s, dh = q.shape
            log_f = jax.nn.log_sigmoid(fg)
            cs = jnp.concatenate([jnp.zeros((1, 1), log_f.dtype), jnp.cumsum(log_f, axis=0)], axis=0)
            neg = jnp.asarray(-0.7 * jnp.finfo(cs.dtype).max, cs.dtype)
            log_d = jnp.where(jnp.tri(s, dtype=bool), (cs - cs.T)[1:, 1:] + ig.T, neg)
            m = jnp.max(log_d, axis=-1, keepdims=True)
            d = jnp.exp(log_d - m)
            c = q @ (k.T / jnp.sqrt(dh)) * d
            n = jnp.maximum(jnp.sum(c, axis=-1, keepdims=True), jnp.exp(-m))
            return c / (n + eps) @ v
        key = jax.random.key(seed)
        ks = jax.random.split(key, 8)
        return {'q': jax.random.normal(ks[0], (B, S, E), jnp.float32), 'k': jax.random.normal(ks[1], (B, S, E), jnp.float32), 'v': jax.random.normal(ks[2], (B, S, E), jnp.float32), 'igate_kernel': jax.random.normal(ks[3], (3 * E, NH), jnp.float32) * 0.02, 'igate_bias': jax.random.normal(ks[4], (NH,), jnp.float32) * 0.1, 'fgate_kernel': jax.random.normal(ks[5], (3 * E, NH), jnp.float32) * 0.02, 'fgate_bias': jnp.linspace(3.0, 6.0, NH, dtype=jnp.float32), 'rms_scale': jax.random.normal(ks[6], (HD,), jnp.float32) * 0.02}
    _L0_xattn_all = _L0_xattn_setup()
    _L0_xattn_in = {k: v for k, v in _L0_xattn_all.items() if k in ('igate_kernel', 'igate_bias', 'fgate_kernel', 'fgate_bias', 'rms_scale')}
    del _L0_xattn_all

    def _L0_ffn_setup():
        import jax, jax.numpy as jnp
        import numpy as np
        N_HEAD, N_ACTIVE, D_MODEL, D_ATTN = (16, 4, 512, 64)
        key = jax.random.key(seed)
        ks = jax.random.split(key, 12)
        s = 0.02
        B, S = (2, 2048)
        return {'x': jax.random.normal(ks[0], (B, S, D_MODEL), dtype=jnp.float32), 'Wq': jax.random.normal(ks[1], (D_MODEL, N_HEAD * D_ATTN), dtype=jnp.float32) * s, 'bq': jnp.zeros((N_HEAD * D_ATTN,), dtype=jnp.float32), 'Wk': jax.random.normal(ks[2], (D_MODEL, N_HEAD * D_ATTN), dtype=jnp.float32) * s, 'bk': jnp.zeros((N_HEAD * D_ATTN,), dtype=jnp.float32), 'Wv': jax.random.normal(ks[3], (D_MODEL, N_HEAD * D_ATTN), dtype=jnp.float32) * s, 'bv': jnp.zeros((N_HEAD * D_ATTN,), dtype=jnp.float32), 'Wr': jax.random.normal(ks[4], (D_MODEL, N_HEAD), dtype=jnp.float32) * s, 'br': jnp.zeros((N_HEAD,), dtype=jnp.float32), 'Wo': jax.random.normal(ks[5], (N_ACTIVE * D_ATTN, D_MODEL), dtype=jnp.float32) * s, 'bo': jnp.zeros((D_MODEL,), dtype=jnp.float32)}
    _L0_ffn_all = _L0_ffn_setup()
    _L0_ffn_in = {k: v for k, v in _L0_ffn_all.items() if k in ('Wq', 'bq', 'Wk', 'bk', 'Wv', 'bv', 'Wr', 'br', 'Wo', 'bo')}
    del _L0_ffn_all
    return {'x': x, 'ctx_1024': ctx_1024, 'L0_attn_Wqkv': _L0_attn_in['Wqkv'], 'L0_attn_Wout': _L0_attn_in['Wout'], 'L0_xattn_igate_kernel': _L0_xattn_in['igate_kernel'], 'L0_xattn_igate_bias': _L0_xattn_in['igate_bias'], 'L0_xattn_fgate_kernel': _L0_xattn_in['fgate_kernel'], 'L0_xattn_fgate_bias': _L0_xattn_in['fgate_bias'], 'L0_xattn_rms_scale': _L0_xattn_in['rms_scale'], 'L0_ffn_Wq': _L0_ffn_in['Wq'], 'L0_ffn_bq': _L0_ffn_in['bq'], 'L0_ffn_Wk': _L0_ffn_in['Wk'], 'L0_ffn_bk': _L0_ffn_in['bk'], 'L0_ffn_Wv': _L0_ffn_in['Wv'], 'L0_ffn_bv': _L0_ffn_in['bv'], 'L0_ffn_Wr': _L0_ffn_in['Wr'], 'L0_ffn_br': _L0_ffn_in['br'], 'L0_ffn_Wo': _L0_ffn_in['Wo'], 'L0_ffn_bo': _L0_ffn_in['bo']}

def reference(x, ctx_1024, L0_attn_Wqkv, L0_attn_Wout, L0_xattn_igate_kernel, L0_xattn_igate_bias, L0_xattn_fgate_kernel, L0_xattn_fgate_bias, L0_xattn_rms_scale, L0_ffn_Wq, L0_ffn_bq, L0_ffn_Wk, L0_ffn_bk, L0_ffn_Wv, L0_ffn_bv, L0_ffn_Wr, L0_ffn_br, L0_ffn_Wo, L0_ffn_bo):
    import jax
    import jax.numpy as jnp

    def _L0_attn_ref(x, Wqkv, Wout):
        import jax, jax.numpy as jnp
        import numpy as np
        B, T, D, H = (4, 1024, 512, 16)
        HEAD_DIM = D // H
        LOCAL_WINDOW = 256

        def _rotate_half(t):
            t1, t2 = jnp.split(t, 2, axis=-1)
            return jnp.concatenate([-t2, t1], axis=-1)

        def _apply_rope(q, k):
            Tq, d = (q.shape[2], q.shape[3])
            half = d // 2
            theta = 1.0 / 10000.0 ** (jnp.arange(half, dtype=jnp.float32) / half)
            pos = jnp.arange(Tq, dtype=jnp.float32)
            freqs = pos[:, None] * theta[None, :]
            freqs = jnp.concatenate([freqs, freqs], axis=-1)
            cos = jnp.cos(freqs)[None, None]
            sin = jnp.sin(freqs)[None, None]
            q = q * cos + _rotate_half(q) * sin
            k = k * cos + _rotate_half(k) * sin
            return (q, k)
        Bx, Tx, C = x.shape
        h, d, w = (H, HEAD_DIM, LOCAL_WINDOW)
        qkv = x @ Wqkv
        q, k, v = jnp.split(qkv, 3, axis=-1)
        q = q.reshape(Bx, Tx, h, d).transpose(0, 2, 1, 3)
        k = k.reshape(Bx, Tx, h, d).transpose(0, 2, 1, 3)
        v = v.reshape(Bx, Tx, h, d).transpose(0, 2, 1, 3)
        q, k = _apply_rope(q, k)
        idx = jnp.arange(Tx)
        dist = idx[None, :] - idx[:, None]
        allowed = (dist <= 0) & (dist >= -(w - 1))
        scores = jnp.einsum('bhqd,bhkd->bhqk', q, k) / jnp.sqrt(jnp.float32(d))
        scores = jnp.where(allowed[None, None], scores, -jnp.inf)
        weights = jax.nn.softmax(scores, axis=-1)
        out = jnp.einsum('bhqk,bhkd->bhqd', weights, v)
        out = out.transpose(0, 2, 1, 3).reshape(Bx, Tx, C)
        return out @ Wout

    def _L0_xattn_ref(q, k, v, igate_kernel, igate_bias, fgate_kernel, fgate_bias, rms_scale):
        import jax, jax.numpy as jnp
        import numpy as np
        B, S, E, NH = (2, 1024, 512, 4)
        HD = E // NH

        def _mlstm_head(q, k, v, ig, fg, eps=1e-06):
            s, dh = q.shape
            log_f = jax.nn.log_sigmoid(fg)
            cs = jnp.concatenate([jnp.zeros((1, 1), log_f.dtype), jnp.cumsum(log_f, axis=0)], axis=0)
            neg = jnp.asarray(-0.7 * jnp.finfo(cs.dtype).max, cs.dtype)
            log_d = jnp.where(jnp.tri(s, dtype=bool), (cs - cs.T)[1:, 1:] + ig.T, neg)
            m = jnp.max(log_d, axis=-1, keepdims=True)
            d = jnp.exp(log_d - m)
            c = q @ (k.T / jnp.sqrt(dh)) * d
            n = jnp.maximum(jnp.sum(c, axis=-1, keepdims=True), jnp.exp(-m))
            return c / (n + eps) @ v
        b, s, e = q.shape
        nh = igate_kernel.shape[1]
        hd = e // nh
        gate_in = jnp.concatenate((q, k, v), axis=-1)
        ig = (gate_in @ igate_kernel + igate_bias).swapaxes(-1, -2)[..., None]
        fg = (gate_in @ fgate_kernel + fgate_bias).swapaxes(-1, -2)[..., None]
        qh = q.reshape(b, s, nh, hd).swapaxes(1, 2)
        kh = k.reshape(b, s, nh, hd).swapaxes(1, 2)
        vh = v.reshape(b, s, nh, hd).swapaxes(1, 2)
        h = jax.vmap(jax.vmap(_mlstm_head))(qh, kh, vh, ig, fg)
        var = jnp.mean(jnp.square(h.astype(jnp.float32)), axis=-1, keepdims=True)
        h = (h * jax.lax.rsqrt(var + 1e-06)).astype(h.dtype) * (1.0 + rms_scale)
        return h.swapaxes(1, 2).reshape(b, s, e)

    def _L0_ffn_ref(x, Wq, bq, Wk, bk, Wv, bv, Wr, br, Wo, bo):
        import jax, jax.numpy as jnp
        import numpy as np
        N_HEAD, N_ACTIVE, D_MODEL, D_ATTN = (16, 4, 512, 64)
        B, S, D = x.shape
        H, K, dh = (N_HEAD, N_ACTIVE, D_ATTN)
        dist = jax.nn.softmax(jnp.mean(x @ Wr + br, axis=1), axis=-1)
        top_vals, top_idx = jax.lax.top_k(dist, K)
        sparse = jnp.zeros_like(dist).at[jnp.arange(B)[:, None], top_idx].set(top_vals)
        gates_all = jax.nn.softmax(sparse, axis=1)
        g = jnp.take_along_axis(gates_all, top_idx, axis=1)[:, :, None, None]

        def proj(W, b):
            return (x @ W + b).reshape(B, S, H, dh).transpose(0, 2, 1, 3)
        Q, Kt, V = (proj(Wq, bq), proj(Wk, bk), proj(Wv, bv))
        idx = top_idx[:, :, None, None]
        Qk = jnp.take_along_axis(Q, idx, axis=1) * g
        Kk = jnp.take_along_axis(Kt, idx, axis=1) * g
        Vk = jnp.take_along_axis(V, idx, axis=1) * g
        scores = jnp.einsum('bksd,bktd->bkst', Qk, Kk) / jnp.sqrt(jnp.float32(dh))
        attn = jax.nn.softmax(scores, axis=-1)
        out = jnp.einsum('bkst,bktd->bksd', attn, Vk)
        out = out.transpose(0, 2, 1, 3).reshape(B, S, K * dh)
        return out @ Wo + bo
    x = _layernorm(x + _L0_attn_ref(x, L0_attn_Wqkv, L0_attn_Wout), axis=-1)
    x = _layernorm(x + _L0_xattn_ref(x, ctx_1024, ctx_1024, L0_xattn_igate_kernel, L0_xattn_igate_bias, L0_xattn_fgate_kernel, L0_xattn_fgate_bias, L0_xattn_rms_scale), axis=-1)
    x = _layernorm(x + _L0_ffn_ref(x, L0_ffn_Wq, L0_ffn_bq, L0_ffn_Wk, L0_ffn_bk, L0_ffn_Wv, L0_ffn_bv, L0_ffn_Wr, L0_ffn_br, L0_ffn_Wo, L0_ffn_bo), axis=-1)
    return x

_drawn_inputs = setup_inputs


def setup_inputs(seed=0):
    import zlib

    import numpy as np

    out = dict(_drawn_inputs(seed))
    spreads = {'L0_ffn_bq': (0.0, 2.0),
     'L0_ffn_bk': (0.0, 2.0),
     'L0_ffn_bv': (0.0, 0.8),
     'L0_ffn_br': (0.0, 0.8),
     'L0_ffn_bo': (0.0, 0.1)}
    factors = {'L0_xattn_igate_bias': 64.0,
     'L0_xattn_rms_scale': 4.24,
     'L0_ffn_Wq': 64.0,
     'L0_ffn_Wk': 64.0,
     'L0_ffn_Wv': 8.0,
     'L0_ffn_Wr': 8.0,
     'L0_ffn_Wo': 8.0}
    for name, (base, spread) in spreads.items():
        noise = np.random.default_rng([zlib.crc32(name.encode()), seed]).standard_normal(out[name].shape)
        drawn = base * np.exp(spread * noise) if base else spread * noise
        out[name] = jnp.asarray(drawn.astype(out[name].dtype))
    for name, factor in factors.items():
        out[name] = (out[name] * factor).astype(out[name].dtype)
    return out
```

```python
from concourse import mybir
import concourse.bass as bass
import numpy as np

F32 = mybir.dt.float32
BF16 = mybir.dt.bfloat16
U32 = mybir.dt.uint32
ALU = mybir.AluOpType
ACT = mybir.ActivationFunctionType
AX = mybir.AxisListType

P = 128
NB, T, D = 32, 256, 512
TT, KT = T // P, D // P
HA, DA = 16, D // 16
QUADS = HA // 4
HX = 4
DX = D // HX
HF, KF, DF = 16, 4, 64
CAUSAL = P + T
LN_EPS, MLSTM_EPS, RMS_EPS = 1e-5, 1e-6, 1e-6
MASKED = -1e30
LOWEST = -3e38


class Mark:

    def __init__(self, sem, count):
        self.sem, self.count = sem, count


class Lane:

    def __init__(self, nc, name, counts):
        self.sem, self.counts = nc.alloc_semaphore(name + "_done"), counts
        self.spare = nc.alloc_semaphore(name + "_spare")
        self.part, self.parts, self.seen, self.step = [], [], {}, 0

    def wait(self, *marks):
        for m in marks:
            if m is not None and self.seen.get(m.sem, -1) < m.count:
                self.seen[m.sem] = m.count
                self.part.append((None, m, 0, self.step))

    def do(self, make, *after, mark=True, sem=None, by=1, apart=False):
        queued = len(self.part)
        self.wait(*after)
        if apart and len(self.part) > queued:
            self.part.append((None, None, 0, self.step))
        sem = sem or (self.sem if mark else None)
        self.part.append((make, sem, by, self.step))
        if sem is None:
            return None
        self.counts[sem] = self.counts.get(sem, 0) + by
        return Mark(sem, self.counts[sem])

    def so_far(self):
        return Mark(self.sem, self.counts[self.sem])

    def end_part(self):
        self.parts.append(self.part)
        self.part, self.seen = [], {}

    def run(self, part, engine, turn=None, per_turn=None):
        for make, what, by, step in self.parts[part]:
            if make is None and what is None:
                if turn is not None:
                    engine.sem_inc(self.spare, 1)
            elif make is None:
                engine.wait_ge(what.sem, what.count if turn is None or what.sem not in per_turn else turn * per_turn[what.sem] + what.count)
            else:
                made = make(step if turn is None else turn + step)
                if what is not None:
                    made.then_inc(what, by)


def constants():
    half = DA // 2
    theta = (1.0 / 10000.0 ** (np.arange(half, dtype=np.float32) / np.float32(half))).astype(np.float32)
    freqs = (theta[:, None] * np.arange(T, dtype=np.float32)[None, :]).astype(np.float32)
    cos = np.tile(np.cos(freqs), (2 * P // DA, 1))
    sin = np.tile(np.concatenate([-np.sin(freqs), np.sin(freqs)]), (P // DA, 1))
    root = np.float32(1.0 / np.sqrt(DA))
    eye = np.eye(P, dtype=np.float32)
    upto = np.triu(np.ones((P, P), np.float32))
    neg = np.zeros((P, HX, P), np.float32)
    for h in range(HX):
        neg[h, h, :] = -1.0
    parts = {"cos_q": cos * root, "sin_q": sin * root, "cos_k": cos, "sin_k": sin, "eye": eye,
             "upto": upto, "neg": neg.reshape(P, HX * P), "ones": np.ones((P, P), np.float32),
             "mask": np.where(upto.T > 0, 0.0, MASKED)}
    where, at = {}, 0
    for name, a in parts.items():
        where[name] = (at, at + a.shape[1])
        at += a.shape[1]
    return np.concatenate([a.astype(np.float32) for a in parts.values()], axis=1), where


def build(nc, x, ctx, wqkv, wout, igk, igb, fgk, fgb, rms, wq, bq, wk, bk, wv, bv, wr, br, wo, bo, out):
    counts = {}
    pe, act, dve, pool, sp = lanes = [Lane(nc, n, counts) for n in ("pe", "act", "dve", "pool", "sp")]
    s_setup, s_x, s_ctx, s_w, s_out = (nc.alloc_semaphore(n) for n in ("setup_loaded", "x_loaded", "ctx_loaded", "weights_picked", "out_stored"))

    def sb(name, shape, dt=F32):
        return nc.alloc_sbuf_tensor(name, shape, dt).ap()

    table, where = constants()
    const = sb("const", [P, table.shape[1]])
    c = {n: const[:, a:b] for n, (a, b) in where.items()}
    eye, ones, upto = c["eye"], c["ones"], c["upto"]
    neg_pick = c["neg"].rearrange("p (h n) -> p h n", h=HX)
    eye_bf = sb("eye_bf", [P, P], BF16)
    mask_bf = sb("mask_bf", [P, P], BF16)
    wqkv_s = sb("wqkv_s", [P, KT, 3 * D])
    wout_s = sb("wout_s", [P, KT, D])
    wgate_q = sb("wgate_q", [P, KT, 2 * HX])
    wgate_k = sb("wgate_k", [P, KT, 2 * HX])
    wgate_v = sb("wgate_v", [P, KT, 2 * HX])
    gate_bias = sb("gate_bias", [P, 2 * HX])
    rms_w = sb("rms_w", [P, DX])
    bias_col = sb("bias_col", [P, 2, HF])
    wr_s = sb("wr_s", [P, KT, HF])
    br_s = sb("br_s", [1, HF])
    wo_s = sb("wo_s", [P, KF * DF // P, D])
    bo_s = sb("bo_s", [P, D])
    minus_half = sb("minus_half", [P, 8])

    x_tok = sb("x_tok", [P, TT, D])
    x_res = sb("x_res", [P, TT, D])
    x_t = sb("x_t", [P, KT, T])
    qk_raw = [sb(f"qk_raw{i}", [P, 2, T]) for i in range(2)]
    qk_rot = [sb(f"qk_rot{i}", [P, 2, T]) for i in range(2)]
    qk = sb("qk", [P, 2 * QUADS, T])
    v_a = sb("v_a", [P, TT, D])
    neg_max = [sb(f"neg_max{i}", [P, 2, TT]) for i in range(2)]
    p_sum = [sb(f"p_sum{i}", [P, 2, TT]) for i in range(2)]
    p_rec = [sb(f"p_rec{i}", [P, 2, TT]) for i in range(2)]
    p_a = [sb(f"p_a{i}", [P, 2, CAUSAL]) for i in range(2)]
    p_t = sb("p_t", [P, 4, CAUSAL])
    att_t = x_t
    y_a = x_res
    x1 = sb("x1", [P, TT, D])
    ctx1 = sb("ctx1", [P, TT, HX, DX + 1])
    x1_t = sb("x1_t", [P, KT, T])
    ctx_t = sb("ctx_t", [P, KT, T])
    gate = sb("gate", [P, TT, 2 * HX])
    g_abs, g_exp, g_ln, log_f, cum_f, a_col, m_col, em = (sb(n, [P, TT, HX]) for n in ("g_abs", "g_exp", "g_ln", "log_f", "cum_f", "a_col", "m_col", "em"))
    a_row = sb("a_row", [HX, T])
    m_row = sb("m_row", [HX, T])
    decay = sb("decay", [P, HX, CAUSAL])
    c_t = decay
    h_raw = sb("h_raw", [P, TT, HX, DX + 1])
    h_sq = sb("h_sq", [P, TT, HX, DX])
    h_ssq, h_den, h_fac = (sb(n, [P, TT, HX]) for n in ("h_ssq", "h_den", "h_fac"))
    y_b = h_sq.rearrange("p t h n -> p t (h n)")
    x2 = sb("x2", [P, TT, D])
    x2_t = sb("x2_t", [P, KT, T])
    x_sum = sb("x_sum", [P, KT])
    r_lg, r_e, r_dist = (sb(n, [1, HF]) for n in ("r_lg", "r_e", "r_dist"))
    r_top, r_dtop = (sb(n, [1, 8]) for n in ("r_top", "r_dtop"))
    r_idx = sb("r_idx", [1, 8], U32)
    r_s = sb("r_s", [1, 8])
    r_eg = sb("r_eg", [1, KF])
    r_g = sb("r_g", [1, 2 * KF])
    g_bc = sb("g_bc", [P, 2 * KF])
    w_sel = sb("w_sel", [P, KT, 3, KF, DF])
    bv_sel = sb("bv_sel", [P, KF * DF])
    b_sel = sb("b_sel", [P, 2, KF // 2])
    q_f = sb("q_f", [P, 2, T])
    k_f = sb("k_f", [P, 2, T])
    v_f = sb("v_f", [P, TT, KF * DF])
    f_max = sb("f_max", [P, KF, TT])
    f_bias = sb("f_bias", [P, KF, TT])
    f_sum = sb("f_sum", [P, KF, TT])
    f_rec = sb("f_rec", [P, KF, TT])
    p_f = [sb(f"p_f{i}", [P, TT, T]) for i in range(2)]
    pt_f = [sb(f"pt_f{i}", [P, TT, T]) for i in range(2)]
    att_f = sb("att_f", [P, 2, T])
    x2_bo = sb("x2_bo", [P, TT, D])
    y_c = x2_bo
    y_out = sb("y_out", [P, TT, D])
    ln = {s: [sb(f"ln_{n}_{s}", [P, TT, w]) for n, w in (("stat", 6), ("mv", 2), ("rstd", 1), ("shift", 1))] for s in "abc"}

    ps_s = nc.alloc_psum_tensor("ps_s", [P, 4, D], F32).ap()
    ps_t = nc.alloc_psum_tensor("ps_t", [P, D], F32).ap()
    ps_o = nc.alloc_psum_tensor("ps_o", [P, 2, T], F32).ap()
    ps_g = [nc.alloc_psum_tensor(f"ps_g{i}", [P, D], F32).ap() for i in range(2)]
    free = {}
    g_turn = [0]

    def g_take():
        i = g_turn[0] % 2
        g_turn[0] += 1
        return ps_g[i], f"g{i}", free.get(f"g{i}")

    def mm(o, l, r, start, stop, *after, mark=False):
        return pe.do(lambda s: nc.tensor.matmul(o, l, r, start=start, stop=stop), *after, mark=mark)

    def tr(o, i, ident, *after, mark=False):
        return pe.do(lambda s: nc.tensor.transpose(o, i, ident), *after, mark=mark, apart=i.shape[0] < P)

    def A(o, i, f, *after, **kw):
        return act.do(lambda s: nc.scalar.activation(o, i, f, **kw), *after)

    def tt(lane, o, a, b, op, *after):
        e = nc.vector if lane is dve else nc.gpsimd
        return lane.do(lambda s: e.tensor_tensor(o, a, b, op), *after)

    def ts(lane, o, a, s1, s2, op0, op1, *after):
        e = nc.vector if lane is dve else nc.gpsimd
        apart = lane is pool
        if op1 is None:
            return lane.do(lambda s: e.tensor_scalar(o, a, s1, None, op0), *after, apart=apart)
        return lane.do(lambda s: e.tensor_scalar(o, a, s1, s2, op0, op1), *after, apart=apart)

    def stt(o, a, sc, b, op0, op1, *after):
        return dve.do(lambda s: nc.vector.scalar_tensor_tensor(o, a, sc, b, op0, op1), *after)

    def red(o, a, op, *after, negate=False):
        return dve.do(lambda s: nc.vector.tensor_reduce(o, a, AX.X, op, negate=negate), *after)

    def copy(lane, o, a, *after):
        if lane is act:
            return act.do(lambda s: nc.scalar.copy(o, a), *after)
        e = nc.vector if lane is dve else nc.gpsimd
        return lane.do(lambda s: e.tensor_copy(o, a), *after)

    def transposed(src, dst, lane, ready, dst_free):
        m = []
        for t in range(TT):
            bank, name, bank_free = g_take()
            for k in range(KT):
                last = tr(bank[:, k * P:(k + 1) * P], src[:, t, k * P:(k + 1) * P], eye, ready, bank_free, mark=k == KT - 1)
            free[name] = copy(lane, dst[:, :, t * P:(t + 1) * P], bank.rearrange("p (k n) -> p k n", k=KT), last, dst_free)
            m.append(free[name])
            yield 500
        return m[-1]

    def norm(part, y, ready):
        stat, mv, rstd, _ = ln[part]
        for t in range(TT):
            m = dve.do(lambda s, t=t: nc.vector.bn_stats(stat[:, t, :], y[:, t, :]), ready[t], free.get("ln" + part))
        for t in range(TT):
            m = dve.do(lambda s, t=t: nc.vector.bn_aggr(mv[:, t, :], stat[:, t, :]), m, apart=True)
        e = ts(pool, rstd[:, :, 0], mv[:, :, 1], LN_EPS, None, ALU.add, None, m, free.get("ln" + part))
        return m, tt(pool, rstd[:, :, 0], rstd[:, :, 0], minus_half[:, 0:TT], ALU.pow, e)

    loads = []

    def load(dst, src, odd=False):
        def make(s):
            if odd:
                with nc.allow_non_contiguous_dma(reason="a few short columns, once"):
                    return nc.sync.dma_start(dst, src)
            return nc.sync.dma_start(dst, src)
        loads.append(sp.do(make, sem=s_setup, by=16))

    col = lambda w: w.rearrange("(k p) n -> p k n", p=P)
    row = lambda b, n: b.unsqueeze(0).to_broadcast([P, n])
    sp.do(lambda s: nc.sync.dma_start(x_tok, x[0].rearrange("(t p) n -> p t n", p=P)), sem=s_x, by=16)
    x_first = Mark(s_x, 16)
    load(const, nc.inline_tensor(table, name="tables").ap())
    load(wqkv_s, col(wqkv))
    load(wout_s, col(wout))
    for i, w in enumerate((wgate_q, wgate_k, wgate_v)):
        for j, g in enumerate((igk, fgk)):
            load(w[:, :, j * HX:(j + 1) * HX], col(g[i * D:(i + 1) * D, :]), odd=True)
    load(gate_bias[:, 0:HX], row(igb, HX))
    load(gate_bias[:, HX:], row(fgb, HX))
    load(rms_w, row(rms, DX))
    for j, b in enumerate((bq, bk)):
        for half in range(2):
            load(bias_col[half * DF:(half + 1) * DF, j, :], b.rearrange("(h d) -> d h", d=DF), odd=True)
    load(wr_s, col(wr))
    load(br_s, br.unsqueeze(0))
    load(wo_s, col(wo))
    load(bo_s, row(bo, D))
    setup = loads[-1]
    for lane in (pe, act):
        lane.wait(setup)
    copy(dve, eye_bf, eye, setup)
    m1 = copy(dve, mask_bf, c["mask"])
    m2 = tt(dve, wgate_k, wgate_k, wgate_v, ALU.add)
    m2 = ts(dve, rms_w, rms_w, 1.0, None, ALU.add, None)
    ts(pool, minus_half, const[:, 0:8], 0.0, -0.5, ALU.mult, ALU.add, setup)
    m3 = pool.do(lambda s: nc.gpsimd.memset(ctx1[:, :, :, DX:], 1.0))
    for lane in (pe, act, dve, pool):
        lane.wait(m1, m2, m3)

    def part_a(first):
        if first:
            x_in = x_first
        else:
            x_in = sp.do(lambda s: nc.sync.dma_start(x_tok, x[s].rearrange("(t p) n -> p t n", p=P)), *free["x_tok"], sem=s_x, by=16)
        kept = copy(act, x_res, x_tok, x_in, free.get("x_res"))
        x_ready = yield from transposed(x_tok, x_t, act, x_in, free.get("x_t"))
        free["x_tok"] = (kept, pe.so_far())
        roped = []
        for u in range(2 * QUADS // 2):
            bank, name, bank_free = g_take()
            for m in range(2):
                for k in range(KT):
                    n = (2 * u + m) * P
                    last = mm(bank[:, m * T:(m + 1) * T], wqkv_s[:, k, n:n + P], x_t[:, k, :], k == 0, k == KT - 1,
                              x_ready, bank_free, mark=k == KT - 1)
            raw, rot, which = qk_raw[u % 2], qk_rot[u % 2], "q" if u < 2 else "k"
            flat = raw.rearrange("p m n -> p (m n)")
            free[name] = r = copy(act, flat, bank, last, free.get(f"qk_raw{u % 2}"))
            cos, sin = (c[w + which].unsqueeze(1).to_broadcast([P, 2, T]) for w in ("cos_", "sin_"))
            s1 = dve.do(lambda s, a=rot, b=raw: nc.vector.stream_shuffle(a.rearrange("p m n -> p (m n)"), b.rearrange("p m n -> p (m n)"), [(i + DA // 2) % DA for i in range(DA)]), r, apart=True)
            s2 = tt(dve, rot, rot, sin, ALU.mult, s1)
            s3 = tt(pool, raw, raw, cos, ALU.mult, r, s1)
            dst = qk[:, 2 * u:2 * u + 2, :]
            roped.append(tt(dve, dst, raw, rot, ALU.add, s2, s3, free.get("qk")))
            free[f"qk_raw{u % 2}"] = roped[-1]
            yield 3500
        for t in range(TT):
            bank, name, bank_free = g_take()
            for k in range(KT):
                last = mm(bank, x_t[:, k, t * P:(t + 1) * P], wqkv_s[:, k, 2 * D:], k == 0, k == KT - 1, bank_free, mark=k == KT - 1)
            free[name] = v_ready = copy(act, v_a[:, t, :], bank, last, free.get("v_a"))
            yield 3500
        free["x_t"] = last

        def scores(p):
            i = p % 2
            for t in range(TT):
                for j in range(2):
                    h = 2 * p + j
                    rows = slice(DA * (h % 4), DA * (h % 4) + DA)
                    o = ps_s[:, 2 * i + j, t * P:t * P + P * (t + 1)]
                    mm(o, qk[rows, h // 4, t * P:(t + 1) * P], qk[rows, QUADS + h // 4, 0:P * (t + 1)], t == 0, False,
                       roped[h // 8], roped[2 + h // 8], free.get(f"s{i}"))
            for j in range(2):
                o = ps_s[:, 2 * i + j, :].rearrange("p (a n) -> p a n", a=2)[:, :, 0:P]
                last = mm(o, eye_bf, mask_bf.unsqueeze(1).to_broadcast([P, 2, P]), False, True, mark=True)
            return last

        def softmax(p, scored):
            i = p % 2
            for t in range(TT):
                src = ps_s[:, 2 * i:2 * i + 2, t * P:t * P + P * (t + 1)]
                m = red(neg_max[i][:, :, t], src, ALU.max, scored, free.get(f"neg_max{i}"), negate=True)
            for j in range(2):
                for t in range(TT):
                    e = A(p_a[i][:, j, t * P:t * P + P * (t + 1)], ps_s[:, 2 * i + j, t * P:t * P + P * (t + 1)], ACT.Exp,
                          m, free.get(f"p_a{i}"), bias=neg_max[i][:, j, t:t + 1], accum_out=p_sum[i][:, j, t:t + 1])
            free[f"s{i}"] = free[f"neg_max{i}"] = e
            r = dve.do(lambda s: nc.vector.reciprocal(p_rec[i], p_sum[i]), e)
            for j in range(2):
                for t in range(TT):
                    v = p_a[i][:, j, t * P:t * P + P * (t + 1)]
                    n = ts(pool, v, v, p_rec[i][:, j, t:t + 1], 1.0, ALU.mult, ALU.mult, r)
            return n

        def turn(p, j, ready):
            i = p % 2
            for n, block in enumerate((0, 1, 2)):
                last = tr(ps_t[:, n * P:(n + 1) * P], p_a[i][:, j, block * P:(block + 1) * P], eye, ready, free.get("t"), mark=n == 2)
            if j == 1:
                free[f"p_a{i}"] = last
            slot = (2 * p + j) % 4
            lane = dve if j else act
            free["t"] = copy(lane, p_t[:, slot, :], ps_t[:, 0:CAUSAL], last, free.get("p_t"))
            return free["t"]

        def attend(q, turned):
            o = ps_o[:, q % 2, :]
            for k in range(TT):
                for j in range(4):
                    h = 4 * q + j
                    strip = slice(DA * j, DA * (j + 1))
                    cols = slice(0, T) if k == 0 else slice(P, T)
                    w = p_t[:, j, 0:T] if k == 0 else p_t[:, j, T:CAUSAL]
                    last = mm(o[strip, cols], v_a[:, k, h * DA:(h + 1) * DA], w, k == 0, k == TT - 1,
                              v_ready, *turned, free.get("o"), mark=k == TT - 1 and j == 3)
            free["p_t"] = last
            free["o"] = copy(dve, att_t[:, q, :], o, last)
            return free["o"]

        pairs = HA // 2
        ready, turned = [None] * pairs, []
        ready[0] = softmax(0, scores(0))
        yield 1500
        for p in range(pairs):
            if p + 1 < pairs:
                scored = scores(p + 1)
                ready[p + 1] = softmax(p + 1, scored)
                if p + 1 == pairs - 1:
                    free["qk"] = scored
                yield 1500
            for j in range(2):
                turned.append(turn(p, j, ready[p]))
                yield 350
            if p % 2:
                attended = attend(p // 2, turned)
                turned = []
                yield 1000
        free["v_a"] = pe.so_far()
        ys = []
        for t in range(TT):
            bank, name, bank_free = g_take()
            for k in range(KT):
                last = mm(bank, att_t[:, k, t * P:(t + 1) * P], wout_s[:, k, :], k == 0, k == KT - 1, attended, bank_free, mark=k == KT - 1)
            free[name] = y = tt(dve, y_a[:, t, :], bank, x_res[:, t, :], ALU.add, last, kept)
            ys.append(y)
            yield 3500
        free["x_t"] = last
        mean, rstd = norm("a", y_a, ys)
        for t in range(TT):
            free["x_res"] = free["lna"] = ts(dve, x1[:, t, :], y_a[:, t, :], ln["a"][1][:, t, 0:1], ln["a"][2][:, t, 0:1], ALU.subtract, ALU.mult,
                                           mean, rstd, free.get("x1_pe"), free.get("x1_dve"))
        done["x1"] = free["x_res"]
        yield 0

    def part_b():
        ctx_dst = [ctx1[:, t, :, 0:DX] for t in range(TT)]
        for t in range(TT):
            ctx_in = sp.do(lambda s, t=t: nc.sync.dma_start(ctx_dst[t], ctx[s - 1, t * P:(t + 1) * P, :].rearrange("p (h n) -> p h n", h=HX)),
                           free.get("ctx1"), sem=s_ctx, by=16)
        x1_in = done["x1"]
        x1_ready = yield from transposed(x1, x1_t, act, x1_in, free.get("x1_t"))
        free["x1_pe"] = pe.so_far()
        for t in range(TT):
            bank, name, bank_free = g_take()
            for h in range(HX):
                last = tr(bank[:, h * P:(h + 1) * P], ctx1[:, t, h, 0:DX], eye, ctx_in, bank_free, mark=h == HX - 1)
            free[name] = ctx_ready = copy(act, ctx_t[:, :, t * P:(t + 1) * P], bank.rearrange("p (k n) -> p k n", k=KT), last, free.get("ctx_t"))
            yield 500
        bank, name, bank_free = g_take()
        for t in range(TT):
            for n, (src, w) in enumerate([(x1_t, wgate_q), (ctx_t, wgate_k)]):
                for k in range(KT):
                    last = mm(bank[:, t * 2 * HX:(t + 1) * 2 * HX], src[:, k, t * P:(t + 1) * P], w[:, k, :], n + k == 0, n == 1 and k == KT - 1,
                              x1_ready, ctx_ready, bank_free, mark=n == 1 and k == KT - 1)
        bias = gate_bias.unsqueeze(1).to_broadcast([P, TT, 2 * HX])
        free[name] = g = tt(dve, gate, bank[:, 0:TT * 2 * HX].rearrange("p (t g) -> p t g", t=TT), bias, ALU.add, last, free.get("gate"))
        yield 3400
        ig, fg = gate[:, :, 0:HX], gate[:, :, HX:]
        m = stt(g_abs, fg, -1.0, fg, ALU.mult, ALU.max, g, free.get("g_abs"))
        m = A(g_exp, g_abs, ACT.Exp, m, scale=-1.0)
        free["g_abs"] = m
        m = A(g_ln, g_exp, ACT.Ln, m, bias=1.0)
        m = stt(log_f, fg, 0.0, g_ln, ALU.min, ALU.subtract, m, free.get("log_f"))
        yield 300
        bank, name, bank_free = g_take()
        mm(bank[:, 0:HX], upto, log_f[:, 0, :], True, True, m, bank_free)
        mm(bank[:, HX:2 * HX], ones, log_f[:, 0, :], True, False)
        last = mm(bank[:, HX:2 * HX], upto, log_f[:, 1, :], False, True, mark=True)
        free["log_f"] = last
        cs = bank[:, 0:TT * HX].rearrange("p (t h) -> p t h", t=TT)
        m = copy(dve, cum_f, cs, last, free.get("cum_f"))
        free[name] = m
        a_ready = tt(dve, a_col, ig, cum_f, ALU.subtract, m, free.get("a_col"))
        free["gate"] = a_ready
        yield 600
        bank, name, bank_free = g_take()
        for t in range(TT):
            last = tr(bank[0:HX, t * P:(t + 1) * P], a_col[:, t, :], eye, a_ready, bank_free, mark=t == TT - 1)
        free[name] = m = copy(dve, a_row, bank[0:HX, 0:T], last)
        m_ready = dve.do(lambda s: nc.vector.tensor_tensor_scan(m_row, a_row, a_row, LOWEST, ALU.max, ALU.max), m, free.get("m_row"))
        yield 300
        for hp in range(HX // 2):
            bank, name, bank_free = g_take()
            for j in range(2):
                last = mm(bank[:, j * T:(j + 1) * T], neg_pick[0:HX, 2 * hp + j, :], m_row, True, True, m_ready, bank_free, mark=j == 1)
            for j in range(2):
                h = 2 * hp + j
                A(decay[:, h, 0:T], bank[:, j * T:j * T + T], ACT.Exp, last, free.get("c_t"), bias=a_col[:, 0, h:h + 1])
                e = A(decay[:, h, T:CAUSAL], bank[:, j * T + P:j * T + T], ACT.Exp, bias=a_col[:, 1, h:h + 1])
            free[name] = e
            v = decay[:, 2 * hp:2 * hp + 2, 0:P]
            w = decay[:, 2 * hp:2 * hp + 2, T:CAUSAL]
            for block in (v, w):
                d = pool.do(lambda s, b=block: nc.gpsimd.affine_select(out=b, in_=b, compare_op=ALU.is_ge, fill=0.0, base=0,
                                                                       pattern=[[0, 2], [1, P]], channel_multiplier=-1), e, apart=True)
            yield 900
        free["a_col"] = e
        bank, name, bank_free = g_take()
        for t in range(TT):
            last = tr(bank[:, t * HX:(t + 1) * HX], m_row[:, t * P:(t + 1) * P], eye[0:HX, 0:HX], m_ready, bank_free, mark=t == TT - 1)
        free["m_row"] = last
        free[name] = m = tt(dve, m_col, bank[:, 0:TT * HX].rearrange("p (t h) -> p t h", t=TT), cum_f, ALU.add, last, free.get("em"))
        free["cum_f"] = m
        em_ready = A(em, m_col, ACT.Exp, m, free.get("em"), scale=-1.0)
        cts = []
        for h in range(HX):
            bank, name, bank_free = g_take()
            mm(bank[:, 0:T], ctx_t[:, h, 0:P], x1_t[:, h, :], True, True, bank_free)
            last = mm(bank[:, T:CAUSAL], ctx_t[:, h, P:T], x1_t[:, h, P:T], True, True, mark=True)
            free[name] = m = stt(c_t[:, h, :], bank[:, 0:CAUSAL], float(DX) ** -0.5, decay[:, h, :], ALU.mult, ALU.mult, last, d)
            cts.append(m)
            yield 650
        free["x1_t"] = free["ctx_t"] = last
        for t in range(TT):
            for hp in range(HX // 2):
                bank, name, bank_free = g_take()
                for j in range(2):
                    h = 2 * hp + j
                    o = bank[:, j * (DX + 1):(j + 1) * (DX + 1)]
                    for k in range(t + 1):
                        l = c_t[:, h, t * P:(t + 1) * P] if k == 0 else c_t[:, h, T:CAUSAL]
                        last = mm(o, l, ctx1[:, k, h, :], k == 0, k == t, cts[h], bank_free, mark=k == t)
                free[name] = hr = copy(act, h_raw[:, t, 2 * hp:2 * hp + 2, :], bank[:, 0:2 * (DX + 1)].rearrange("p (h n) -> p h n", h=2), last, free.get("h_raw"))
                yield 440 * (t + 1)
        free["c_t"] = free["ctx1"] = last
        hv = h_raw[:, :, :, 0:DX]
        m = tt(dve, h_den, h_raw[:, :, :, DX], em, ALU.max, hr, em_ready)
        free["em"] = m
        m = ts(dve, h_den, h_den, MLSTM_EPS, None, ALU.add, None, m)
        m_den = dve.do(lambda s: nc.vector.reciprocal(h_den, h_den), m)
        for t in range(TT):
            q = A(h_sq[:, t], hv[:, t], ACT.Square, hr, free.get("y_b"))
            m = red(h_ssq[:, t], h_sq[:, t], ALU.add, q)
        squared = m
        m = tt(dve, h_ssq, h_ssq, h_den, ALU.mult, m, m_den)
        m = tt(dve, h_ssq, h_ssq, h_den, ALU.mult, m)
        m = ts(dve, h_ssq, h_ssq, 1.0 / DX, RMS_EPS, ALU.mult, ALU.add, m)
        m = tt(pool, h_ssq, h_ssq, minus_half[:, 0:TT * HX].rearrange("p (t h) -> p t h", t=TT), ALU.pow, m)
        m = tt(dve, h_fac, h_ssq, h_den, ALU.mult, m)
        yield 0
        ys = []
        for t in range(TT):
            m1 = tt(pool, h_sq[:, t], hv[:, t], h_fac[:, t].unsqueeze(2).to_broadcast([P, HX, DX]), ALU.mult, m, squared)
            m2 = tt(dve, h_sq[:, t], h_sq[:, t], rms_w.unsqueeze(1).to_broadcast([P, HX, DX]), ALU.mult, m1)
            ys.append(tt(dve, y_b[:, t, :], h_sq[:, t].rearrange("p h n -> p (h n)"), x1[:, t, :], ALU.add, m2, x1_in))
        free["h_raw"] = m1
        free["x1_dve"] = ys[-1]
        mean, rstd = norm("b", y_b, ys)
        yield 0
        for t in range(TT):
            free["y_b"] = free["lnb"] = ts(dve, x2[:, t, :], y_b[:, t, :], ln["b"][1][:, t, 0:1], ln["b"][2][:, t, 0:1], ALU.subtract, ALU.mult,
                                           mean, rstd, free.get("x2_pe"), free.get("x2_pool"))
        done["x2"] = free["y_b"]
        yield 0

    def part_c():
        x2_in = done["x2"]
        x2_ready = yield from transposed(x2, x2_t, act, x2_in, free.get("x2_t"))
        free["x2_pe"] = pe.so_far()
        for t in range(TT):
            with_bo = tt(pool, x2_bo[:, t, :], x2[:, t, :], bo_s, ALU.add, x2_in, free.get("y_c"))
        free["x2_pool"] = with_bo
        m = red(x_sum, x2_t, ALU.add, x2_ready, free.get("x_sum"))
        bank, name, bank_free = g_take()
        for k in range(KT):
            last = mm(bank[0:1, 0:HF], x_sum[:, k:k + 1], wr_s[:, k, :], k == 0, k == KT - 1, m, bank_free, mark=k == KT - 1)
        free["x_sum"] = last
        free[name] = m = stt(r_lg, bank[0:1, 0:HF], 1.0 / T, br_s, ALU.mult, ALU.add, last)
        yield 400
        m = dve.do(lambda s: nc.vector.max(r_top, r_lg), m, apart=True)
        m = ts(dve, r_s[:, 0:1], r_top[:, 0:1], -1.0, None, ALU.mult, None, m)
        m = A(r_e, r_lg, ACT.Exp, m, bias=r_s[:, 0:1], accum_out=r_s[:, 1:2])
        yield 100
        m = dve.do(lambda s: nc.vector.reciprocal(r_s[:, 2:3], r_s[:, 1:2]), m)
        m = ts(dve, r_dist, r_e, r_s[:, 2:3], None, ALU.mult, None, m)
        m = dve.do(lambda s: nc.vector.max(r_dtop, r_dist), m, apart=True)
        picked = dve.do(lambda s: nc.vector.max_index(r_idx, r_dtop, r_dist), m, apart=True)
        m = ts(dve, r_s[:, 3:4], r_dtop[:, 0:1], -1.0, None, ALU.mult, None, m)
        A(r_eg, r_dtop[:, 0:KF], ACT.Exp, m, bias=r_s[:, 3:4], accum_out=r_s[:, 4:5])
        m = A(r_s[:, 5:6], r_dtop[:, 0:1], ACT.Exp, scale=-1.0)
        for k in range(KF):
            half = slice(DF * (k % 2), DF * (k % 2) + DF)

            def gather(s, k=k, half=half):
                h = nc.vector.value_load(r_idx[0:1, k:k + 1], min_val=0, max_val=HF - 1)
                return nc.vector.tensor_copy(b_sel[half, :, k // 2:k // 2 + 1], bias_col[half, :, bass.ds(h, 1)])
            b_picked = dve.do(gather, picked, free.get("b_sel"), apart=True)
            head = []

            def fetch(s, k=k, j=0, head=head):
                if j == 0:
                    head.append(nc.sync.value_load(r_idx[0:1, k:k + 1], min_val=0, max_val=HF - 1) * DF)
                return nc.sync.dma_start(w_sel[:, :, j, k, :], col((wq, wk, wv)[j])[:, :, bass.ds(head[-1], DF)])
            for j in range(3):
                sp.do(lambda s, j=j, f=fetch: f(s, j=j), picked, *free.get("w_sel", ()), sem=s_w, by=16, apart=True)
            w_picked = sp.do(lambda s, k=k, head=head: nc.sync.dma_start(bv_sel[:, k * DF:(k + 1) * DF], bv.unsqueeze(0)[:, bass.ds(head[-1], DF)].to_broadcast([P, DF])),
                             sem=s_w, by=16)
        yield 100
        m = stt(r_s[:, 6:7], r_s[:, 5:6], float(HF - KF), r_s[:, 4:5], ALU.mult, ALU.add, m)
        m = dve.do(lambda s: nc.vector.reciprocal(r_s[:, 7:8], r_s[:, 6:7]), m)
        m = ts(dve, r_g[:, 0:KF], r_eg, r_s[:, 7:8], None, ALU.mult, None, m)
        m = stt(r_g[:, KF:], r_g[:, 0:KF], float(DF) ** -0.5, r_g[:, 0:KF], ALU.mult, ALU.mult, m)
        yield 100
        bank, name, bank_free = g_take()
        last = mm(bank[:, 0:2 * KF], ones[0:1, :], r_g, True, True, m, bank_free, mark=True)
        free[name] = g_ready = copy(dve, g_bc, bank[:, 0:2 * KF], last, free.get("g_bc"))
        yield 200
        for j, dst in enumerate((q_f, k_f)):
            bank, name, bank_free = g_take()
            for m in range(2):
                w = w_sel[:, :, j, 2 * m:2 * m + 2, :].rearrange("p k h d -> p k (h d)")
                for k in range(KT):
                    last = mm(bank[:, m * T:(m + 1) * T], w[:, k, :], x2_t[:, k, :], k == 0, k == KT - 1, w_picked, bank_free, mark=k == KT - 1)
            for m in range(2):
                qk_ready = ts(dve, dst[:, m, :], bank[:, m * T:(m + 1) * T], b_sel[:, j, m:m + 1], None, ALU.add, None, last, b_picked, free.get("qk_f"))
            free[name] = qk_ready
            yield 3500
        free["b_sel"] = qk_ready
        bank, name, bank_free = g_take()
        for t in range(TT):
            for k in range(KT):
                last = mm(bank[:, t * T:(t + 1) * T], x2_t[:, k, t * P:(t + 1) * P], w_sel[:, k, 2].rearrange("p h d -> p (h d)"), k == 0, k == KT - 1, bank_free, mark=k == KT - 1)
        free["x2_t"] = last
        bv_b = bv_sel.unsqueeze(1).to_broadcast([P, TT, KF * DF])
        v_ready = free[name] = tt(dve, v_f, bank.rearrange("p (t n) -> p t n", t=TT), bv_b, ALU.add, last, w_picked, free.get("v_f"))
        free["w_sel"] = (last, v_ready)
        yield 3500

        def scores(k):
            rows = slice(DF * (k % 2), DF * (k % 2) + DF)
            bank, name, bank_free = g_take()
            for t in range(TT):
                last = mm(bank[:, t * T:(t + 1) * T], q_f[rows, k // 2, t * P:(t + 1) * P], k_f[rows, k // 2, :], True, True, qk_ready, bank_free, mark=t == TT - 1)
            free["qk_f"] = last
            m = red(f_max[:, k, :], bank.rearrange("p (t n) -> p t n", t=TT), ALU.max, last)
            m = ts(dve, f_bias[:, k, :], f_max[:, k, :], g_bc[:, KF + k:KF + k + 1], -1.0, ALU.mult, ALU.mult, m, g_ready, free.get(f"f_bias{k}"))
            for t in range(TT):
                e = A(p_f[k % 2][:, t, :], bank[:, t * T:(t + 1) * T], ACT.Exp, m, free.get(f"p_f{k % 2}"), scale=g_bc[:, KF + k:KF + k + 1],
                      bias=f_bias[:, k, t:t + 1], accum_out=f_sum[:, k, t:t + 1])
            free[name] = free[f"f_bias{k}"] = e
            r = dve.do(lambda s: nc.vector.reciprocal(f_rec[:, k, :], f_sum[:, k, :]), e)
            for t in range(TT):
                n = ts(pool, p_f[k % 2][:, t, :], p_f[k % 2][:, t, :], f_rec[:, k, t:t + 1], g_bc[:, k:k + 1], ALU.mult, ALU.mult, r)
            free["g_bc"] = n
            return n

        def turn(k, ready):
            bank, name, bank_free = g_take()
            for kk in range(TT):
                for t in range(TT):
                    last = tr(bank[:, kk * T + t * P:kk * T + (t + 1) * P], p_f[k % 2][:, t, kk * P:(kk + 1) * P], eye, ready, bank_free, mark=t + kk == 2)
            free[f"p_f{k % 2}"] = last
            free[name] = copy(act if k % 2 else dve, pt_f[k % 2].rearrange("p k n -> p (k n)"), bank, last, free.get("pt_f"))
            return free[name]

        ready = [scores(0)]
        yield 900
        turned = []
        for k in range(KF):
            if k + 1 < KF:
                ready.append(scores(k + 1))
                yield 900
            turned.append(turn(k, ready[k]))
            yield 450
            if k % 2:
                bank, name, bank_free = g_take()
                for kk in range(TT):
                    for j in range(2):
                        h = k - 1 + j
                        last = mm(bank[DF * j:DF * (j + 1), 0:T], v_f[:, kk, h * DF:(h + 1) * DF], pt_f[j][:, kk, :], kk == 0, kk == TT - 1,
                                  v_ready, *turned, bank_free, mark=kk + j == 2)
                free["pt_f"] = last
                free[name] = attended = copy(dve, att_f[:, k // 2, :], bank[:, 0:T], last, free.get("att_f"))
                turned = []
                yield 900
        free["v_f"] = last
        ys = []
        for t in range(TT):
            bank, name, bank_free = g_take()
            for k in range(2):
                last = mm(bank, att_f[:, k, t * P:(t + 1) * P], wo_s[:, k, :], k == 0, k == 1, attended, bank_free, mark=k == 1)
            free[name] = y = tt(dve, y_c[:, t, :], bank, x2_bo[:, t, :], ALU.add, last, with_bo)
            ys.append(y)
            yield 1800
        free["att_f"] = last
        mean, rstd = norm("c", y_c, ys)
        yield 0
        _, mv, rs, shift = ln["c"]
        m = stt(shift[:, :, 0], mv[:, :, 0], -1.0, rs[:, :, 0], ALU.mult, ALU.mult, mean, rstd, free.get("y_c"))
        for t in range(TT):
            e = A(y_out[:, t, :], y_c[:, t, :], ACT.Identity, m, free.get("y_out"), scale=rs[:, t, 0:1], bias=shift[:, t, 0:1])
        free["y_c"] = free["lnc"] = e
        free["y_out"] = act.do(lambda s: nc.scalar.dma_start(out[s - 2].rearrange("(t p) n -> p t n", p=P), y_out), e, sem=s_out, by=16)
        yield 0

    done = {}
    SPAN = {"a": 52000.0, "b": 20000.0, "c": 26000.0}

    def step(parts, first=False):
        running = {n: {"a": lambda: part_a(first), "b": part_b, "c": part_c}[n]() for n in parts}
        g_turn[0] = 0
        at = {n: {"c": -0.04, "b": -0.02, "a": 0.0}[n] for n in parts}
        while running:
            n = min(running, key=lambda n: at[n])
            try:
                at[n] += (next(running[n]) + 200) / SPAN[n]
            except StopIteration:
                del running[n]

    def end_part():
        for lane in lanes:
            lane.end_part()

    def next_step():
        for lane in lanes:
            lane.step += 1

    LEAD = 3
    TURNS = NB - LEAD
    for parts in ("a", "ab", "abc"):
        step(parts, first=parts == "a")
        next_step()
    end_part()
    before = dict(counts)
    step("abc")
    end_part()
    per_turn = {s: n - before[s] for s, n in counts.items() if n > before[s]}

    def last_turn(m):
        if isinstance(m, tuple):
            return tuple(last_turn(n) for n in m)
        if m is None or m.count <= before.get(m.sem, 0):
            return m
        return Mark(m.sem, m.count + per_turn[m.sem] * (TURNS - 1))
    for marks in (free, done):
        for name, m in marks.items():
            marks[name] = last_turn(m)
    for s, n in per_turn.items():
        counts[s] += n * (TURNS - 1)
    for lane in lanes:
        lane.step += TURNS
    for parts in ("bc", "c"):
        step(parts)
        next_step()
    sp.wait(free["y_out"])
    end_part()

    def program(lane):
        def run(engine):
            lane.run(0, engine)
            with engine.Fori(0, TURNS) as turn:
                lane.run(1, engine, turn, per_turn)
            lane.run(2, engine)
        return run

    with nc.Block() as block:
        block.tensor(program(pe))
        block.scalar(program(act))
        block.vector(program(dve))
        block.gpsimd(program(pool))
        block.sync(program(sp))


INPUTS = ["x", "ctx_1024", "L0_attn_Wqkv", "L0_attn_Wout", "L0_xattn_igate_kernel", "L0_xattn_igate_bias",
          "L0_xattn_fgate_kernel", "L0_xattn_fgate_bias", "L0_xattn_rms_scale", "L0_ffn_Wq", "L0_ffn_bq", "L0_ffn_Wk",
          "L0_ffn_bk", "L0_ffn_Wv", "L0_ffn_bv", "L0_ffn_Wr", "L0_ffn_br", "L0_ffn_Wo", "L0_ffn_bo"]


def kernel(**inputs):
    import concourse.bacc as bacc
    from concourse.bass_utils import run_bass_kernel_spmd

    nc = bacc.Bacc("TRN2", target_bir_lowering=False, num_devices=1)
    arrays, args = {}, []
    for name in INPUTS:
        a = np.ascontiguousarray(inputs[name])
        arrays["in_" + name] = a
        args.append(nc.dram_tensor("in_" + name, a.shape, mybir.dt.from_np(a.dtype), kind="ExternalInput").ap())
    out = nc.dram_tensor("out", (NB, T, D), F32, kind="ExternalOutput").ap()
    build(nc, *args, out)
    r = run_bass_kernel_spmd(nc, [arrays], core_ids=[0])
    return r.results[0]["out"]
```

```python
from concourse import mybir
import concourse.bass as bass
import numpy as np

F32 = mybir.dt.float32
BF16 = mybir.dt.bfloat16
F32R = mybir.dt.float32r
U32 = mybir.dt.uint32
ALU = mybir.AluOpType
ACT = mybir.ActivationFunctionType
AX = mybir.AxisListType

P = 128
NB, T, D = 32, 256, 512
TT, KT = T // P, D // P
HA, DA = 16, D // 16
QUADS = HA // 4
HX = 4
DX = D // HX
HF, KF, DF = 16, 4, 64
CAUSAL = P + T
LN_EPS, MLSTM_EPS, RMS_EPS = 1e-5, 1e-6, 1e-6
MASKED = -1e30
LOWEST = -3e38
ORDER = "ccbabaccbbccaacbacccaaaacbcaabaabcaacbcabaaabaabbbaccacaabbaabaaccaacbbacaaacabcccabcaa"


class Mark:

    def __init__(self, sem, count):
        self.sem, self.count = sem, count


class Lane:

    def __init__(self, nc, name, counts):
        self.sem, self.counts = nc.alloc_semaphore(name + "_done"), counts
        self.spare = nc.alloc_semaphore(name + "_spare")
        self.part, self.parts, self.seen, self.step = [], [], {}, 0

    def wait(self, *marks):
        for m in marks:
            if m is not None and self.seen.get(m.sem, -1) < m.count:
                self.seen[m.sem] = m.count
                self.part.append((None, m, 0, self.step))

    def do(self, make, *after, mark=True, sem=None, by=1, apart=False):
        for m in after:
            queued = len(self.part)
            self.wait(m)
            if apart and len(self.part) > queued:
                self.part.append((None, None, 0, self.step))
        sem = sem or (self.sem if mark else None)
        self.part.append((make, sem, by, self.step))
        if sem is None:
            return None
        self.counts[sem] = self.counts.get(sem, 0) + by
        return Mark(sem, self.counts[sem])

    def so_far(self):
        return Mark(self.sem, self.counts[self.sem])

    def end_part(self):
        self.parts.append(self.part)
        self.part, self.seen = [], {}

    def run(self, part, engine, turn=None, per_turn=None):
        for make, what, by, step in self.parts[part]:
            if make is None and what is None:
                if turn is not None:
                    engine.sem_inc(self.spare, 1)
            elif make is None:
                engine.wait_ge(what.sem, what.count if turn is None or what.sem not in per_turn else turn * per_turn[what.sem] + what.count)
            else:
                made = make(step if turn is None else turn + step)
                if what is not None:
                    made.then_inc(what, by)


def constants():
    half = DA // 2
    theta = (1.0 / 10000.0 ** (np.arange(half, dtype=np.float32) / np.float32(half))).astype(np.float32)
    freqs = (theta[:, None] * np.arange(T, dtype=np.float32)[None, :]).astype(np.float32)
    cos = np.tile(np.cos(freqs), (2 * P // DA, 1))
    sin = np.tile(np.concatenate([-np.sin(freqs), np.sin(freqs)]), (P // DA, 1))
    root = np.float32(1.0 / np.sqrt(DA))
    eye = np.eye(P, dtype=np.float32)
    upto = np.triu(np.ones((P, P), np.float32))
    parts = {"cos_q": cos * root, "sin_q": sin * root, "cos_k": cos, "sin_k": sin, "eye": eye,
             "upto": upto, "minus_eye": -eye[:, 0:HX], "ones": np.ones((P, P), np.float32),
             "mask": np.where(upto.T > 0, 0.0, MASKED)}
    where, at = {}, 0
    for name, a in parts.items():
        where[name] = (at, at + a.shape[1])
        at += a.shape[1]
    return np.concatenate([a.astype(np.float32) for a in parts.values()], axis=1), where


def build(nc, x, ctx, wqkv, wout, igk, igb, fgk, fgb, rms, wq, bq, wk, bk, wv, bv, wr, br, wo, bo, out):
    counts = {}
    pe, act, dve, pool, sp = lanes = [Lane(nc, n, counts) for n in ("pe", "act", "dve", "pool", "sp")]
    s_setup, s_x, s_ctx, s_w, s_out, *s_stage = (nc.alloc_semaphore(n) for n in ("setup_loaded", "x_loaded", "ctx_loaded", "weights_picked", "out_stored", *(f"staged{i}" for i in range(6))))

    def sb(name, shape, dt=F32):
        return nc.alloc_sbuf_tensor(name, shape, dt).ap()

    table, where = constants()
    const = sb("const", [P, table.shape[1]])
    c = {n: const[:, a:b] for n, (a, b) in where.items()}
    eye, ones, upto = c["eye"], c["ones"], c["upto"]
    minus_eye = c["minus_eye"]
    eye_bf = sb("eye_bf", [P, P], BF16)
    mask_bf = sb("mask_bf", [P, P], BF16)

    def halves(name, shape):
        return [sb(f"{name}_{part}", shape, F32R) for part in ("hi", "lo")]

    wqkv_s = halves("wqkv", [P, KT, 3 * D])
    wout_s = halves("wout", [P, KT, D])
    wgate_q = sb("wgate_q", [P, KT, 2 * HX])
    wgate_k = sb("wgate_k", [P, KT, 2 * HX])
    wgate_v = sb("wgate_v", [P, KT, 2 * HX])
    gate_bias = sb("gate_bias", [P, 2 * HX])
    rms_w = sb("rms_w", [P, DX])
    bias_col = sb("bias_col", [P, 2, HF])
    wr_s = sb("wr_s", [P, KT, HF])
    br_s = sb("br_s", [1, HF])
    wo_s = halves("wo", [P, KF * DF // P, D])
    bo_s = sb("bo_s", [P, D])
    minus_half = sb("minus_half", [P, 8])

    x_tok = sb("x_tok", [P, TT, D])
    x_res = sb("x_res", [P, TT, D])
    x_t = halves("x_t", [P, KT, T])
    qk = sb("qk", [P, 2 * QUADS, T])
    v_a = sb("v_a", [P, TT, D])
    neg_max = [sb(f"neg_max{i}", [P, 2, TT]) for i in range(2)]
    p_sum = [sb(f"p_sum{i}", [P, 2, TT]) for i in range(2)]
    p_rec = [sb(f"p_rec{i}", [P, 2, TT]) for i in range(2)]
    p_a = [sb(f"p_a{i}", [P, 2, CAUSAL]) for i in range(2)]
    p_t = sb("p_t", [P, 4, CAUSAL])
    qk_raw = [p_t.rearrange("p h n -> p (h n)")[:, i * 2 * T:(i + 1) * 2 * T].rearrange("p (m n) -> p m n", m=2) for i in range(2)]
    qk_rot = [p_a[i].rearrange("p h n -> p (h n)")[:, 0:2 * T].rearrange("p (m n) -> p m n", m=2) for i in range(2)]
    att_t = x_t
    y_a = x_res
    x1 = sb("x1", [P, TT, D])
    ctx1 = sb("ctx1", [P, TT, HX, DX + 1])
    h_raw = sb("h_raw", [P, TT, HX, DX + 1])
    x1_t = h_raw.rearrange("p t h n -> p (t h n)")[:, 0:KT * T].rearrange("p (k n) -> p k n", k=KT)
    ctx_t = sb("ctx_t", [P, KT, T])
    gate = sb("gate", [P, TT, 2 * HX])
    g_abs, g_exp, g_ln, log_f, cum_f, a_col, m_col, em = (sb(n, [P, TT, HX]) for n in ("g_abs", "g_exp", "g_ln", "log_f", "cum_f", "a_col", "m_col", "em"))
    a_row = sb("a_row", [HX, T])
    m_row = sb("m_row", [HX, T])
    decay = sb("decay", [P, HX, CAUSAL])
    c_t = decay
    h_sq = ctx_t.rearrange("p k (t n) -> p (k t n)", t=TT).rearrange("p (t h n) -> p t h n", t=TT, h=HX)
    h_ssq, h_den, h_fac = (sb(n, [P, TT, HX]) for n in ("h_ssq", "h_den", "h_fac"))
    y_b = h_sq.rearrange("p t h n -> p t (h n)")
    x2 = sb("x2", [P, TT, D])
    x2_t = halves("x2_t", [P, KT, T])
    x_sum = sb("x_sum", [P, TT, KT])
    r_lg, r_e, r_dist = (sb(n, [1, HF]) for n in ("r_lg", "r_e", "r_dist"))
    r_top, r_dtop = (sb(n, [1, 8]) for n in ("r_top", "r_dtop"))
    r_idx = sb("r_idx", [1, 8], U32)
    r_s = sb("r_s", [1, 8])
    r_eg = sb("r_eg", [1, KF])
    r_g = sb("r_g", [1, 2 * KF])
    g_bc = sb("g_bc", [P, 2 * KF])
    w_sel = halves("w_sel", [P, KT, 3, KF, DF])
    bv_sel = sb("bv_sel", [P, KF * DF])
    b_sel = sb("b_sel", [P, 2, KF // 2])
    q_f = sb("q_f", [P, 2, T])
    k_f = sb("k_f", [P, 2, T])
    v_f = sb("v_f", [P, TT, KF * DF])
    f_max = sb("f_max", [P, KF, TT])
    f_bias = sb("f_bias", [P, KF, TT])
    f_sum = sb("f_sum", [P, KF, TT])
    f_rec = sb("f_rec", [P, KF, TT])
    p_all = sb("p_all", [P, 2, TT, T])
    pt_all = sb("pt_all", [P, 2, TT, T])
    p_f = [p_all[:, i] for i in range(2)]
    pt_f = [pt_all[:, i] for i in range(2)]
    att_f = [h[:, 0:2, :] for h in x2_t]
    x2_bo = sb("x2_bo", [P, TT, D])
    y_c = x2_bo
    y_out = sb("y_out", [P, TT, D])
    w_raw = [p_all.rearrange("p i t n -> p (i t n)"), pt_all.rearrange("p i t n -> p (i t n)"), y_out.rearrange("p t n -> p (t n)")]
    w_raw = [w.rearrange("p (k h d) -> p k h d", k=KT, h=KF) for w in w_raw]
    ln = {s: [sb(f"ln_{n}_{s}", [P, TT, w]) for n, w in (("stat", 6), ("mv", 2), ("rstd", 1), ("shift", 1))] for s in "abc"}

    ps_s = nc.alloc_psum_tensor("ps_s", [P, 4, D], F32).ap()
    RING = 4
    ps_g = [nc.alloc_psum_tensor(f"ps_g{i}", [P, D], F32).ap() for i in range(RING)]
    free = {}
    g_turn = [0]

    def g_take():
        i = g_turn[0] % RING
        g_turn[0] += 1
        return ps_g[i], f"g{i}", free.get(f"g{i}")

    def mm(o, l, r, start, stop, *after, mark=False):
        return pe.do(lambda s: nc.tensor.matmul(o, l, r, start=start, stop=stop), *after, mark=mark)

    def mm3(o, l, r, first, last, *after, mark=False):
        mm(o, l[0], r[0], first, False, *after)
        mm(o, l[0], r[1], False, False)
        return mm(o, l[1], r[0], False, last, mark=mark)

    def part(pair, *at):
        return [h[at] for h in pair]

    def split(dst, src, bank, *after):
        a = copy(act, dst[0], src, *after)
        m = tt(dve, dst[1], src, dst[0].bitcast(F32), ALU.subtract, a)
        if bank:
            free[bank] = m
        return m

    def tr(o, i, ident, *after, mark=False):
        return pe.do(lambda s: nc.tensor.transpose(o, i, ident), *after, mark=mark, apart=i.shape[0] < P)

    def A(o, i, f, *after, **kw):
        return act.do(lambda s: nc.scalar.activation(o, i, f, **kw), *after)

    def tt(lane, o, a, b, op, *after):
        e = nc.vector if lane is dve else nc.gpsimd
        return lane.do(lambda s: e.tensor_tensor(o, a, b, op), *after)

    def ts(lane, o, a, s1, s2, op0, op1, *after):
        e = nc.vector if lane is dve else nc.gpsimd
        apart = lane is pool
        if op1 is None:
            return lane.do(lambda s: e.tensor_scalar(o, a, s1, None, op0), *after, apart=apart)
        return lane.do(lambda s: e.tensor_scalar(o, a, s1, s2, op0, op1), *after, apart=apart)

    def stt(o, a, sc, b, op0, op1, *after):
        return dve.do(lambda s: nc.vector.scalar_tensor_tensor(o, a, sc, b, op0, op1), *after)

    def red(o, a, op, *after, negate=False):
        return dve.do(lambda s: nc.vector.tensor_reduce(o, a, AX.X, op, negate=negate), *after)

    def copy(lane, o, a, *after):
        if lane is act:
            return act.do(lambda s: nc.scalar.copy(o, a), *after)
        e = nc.vector if lane is dve else nc.gpsimd
        return lane.do(lambda s: e.tensor_copy(o, a), *after)

    def transposed(src, dst, ready, dst_free, sums=None):
        m = []
        for t in range(TT):
            bank, name, bank_free = g_take()
            for k in range(KT):
                last = tr(bank[:, k * P:(k + 1) * P], src[:, t, k * P:(k + 1) * P], eye, ready, bank_free, mark=k == KT - 1)
            blocks = bank.rearrange("p (k n) -> p k n", k=KT)
            if isinstance(dst, list):
                m.append(split(part(dst, slice(None), slice(None), slice(t * P, (t + 1) * P)), blocks, name, last, dst_free))
            else:
                m.append(copy(act, dst[:, :, t * P:(t + 1) * P], blocks, last, dst_free))
            if sums is not None:
                m[-1] = red(sums[:, t, :], blocks, ALU.add, m[-1], free.get("x_sum"))
            free[name] = m[-1]
            yield
        return m[-1]

    def norm(which, y, ready):
        stat, mv, rstd, _ = ln[which]
        for t in range(TT):
            m = dve.do(lambda s, t=t: nc.vector.bn_stats(stat[:, t, :], y[:, t, :]), ready[t], free.get("ln" + which))
        for t in range(TT):
            m = dve.do(lambda s, t=t: nc.vector.bn_aggr(mv[:, t, :], stat[:, t, :]), m, apart=True)
        e = ts(pool, rstd[:, :, 0], mv[:, :, 1], LN_EPS, None, ALU.add, None, m, free.get("ln" + which))
        return m, tt(pool, rstd[:, :, 0], rstd[:, :, 0], minus_half[:, 0:TT], ALU.pow, e)

    loads = []

    def load(dst, src, odd=False):
        def make(s):
            if odd:
                with nc.allow_non_contiguous_dma(reason="a few short columns, once"):
                    return nc.sync.dma_start(dst, src)
            return nc.sync.dma_start(dst, src)
        loads.append(sp.do(make, sem=s_setup, by=16))

    col = lambda w: w.rearrange("(k p) n -> p k n", p=P)
    row = lambda b, n: b.unsqueeze(0).to_broadcast([P, n])
    sp.do(lambda s: nc.sync.dma_start(x_tok, x[0].rearrange("(t p) n -> p t n", p=P)), sem=s_x, by=16)
    x_first = Mark(s_x, 16)
    load(const, nc.inline_tensor(table, name="tables").ap())
    for i, w in enumerate((wgate_q, wgate_k, wgate_v)):
        for j, g in enumerate((igk, fgk)):
            load(w[:, :, j * HX:(j + 1) * HX], col(g[i * D:(i + 1) * D, :]), odd=True)
    load(gate_bias[:, 0:HX], row(igb, HX))
    load(gate_bias[:, HX:], row(fgb, HX))
    load(rms_w, row(rms, DX))
    for j, b in enumerate((bq, bk)):
        for half in range(2):
            load(bias_col[half * DF:(half + 1) * DF, j, :], b.rearrange("(h d) -> d h", d=DF), odd=True)
    load(wr_s, col(wr))
    load(br_s, br.unsqueeze(0))
    load(bo_s, row(bo, D))
    setup = loads[-1]
    stages = [p_all.rearrange("p i t n -> p (i t n)"), pt_all.rearrange("p i t n -> p (i t n)"), y_out.rearrange("p t n -> p (t n)"),
              x2_bo.rearrange("p t n -> p (t n)"), x2.rearrange("p t n -> p (t n)"), x1.rearrange("p t n -> p (t n)")]
    pieces = [(col(wqkv)[:, 2 * k:2 * k + 2, j * D:(j + 1) * D], part(wqkv_s, slice(None), slice(2 * k, 2 * k + 2), slice(j * D, (j + 1) * D))) for j in range(3) for k in range(2)]
    pieces += [(col(wout)[:, 2 * k:2 * k + 2, :], part(wout_s, slice(None), slice(2 * k, 2 * k + 2), slice(None))) for k in range(2)]
    pieces += [(col(wo), wo_s)]
    stage_free = [None] * len(stages)
    staged = []
    for n, (src, dst) in enumerate(pieces):
        i = n % len(stages)
        buf = stages[i].rearrange("p (k n) -> p k n", k=2)
        m = sp.do(lambda s, b=buf, src=src: nc.sync.dma_start(b, src), stage_free[i], sem=s_stage[i], by=16)
        stage_free[i] = split(dst, buf, None, m)
        staged.append(stage_free[i])
    for lane in (pe, act):
        lane.wait(setup)
    copy(dve, eye_bf, eye, setup)
    m1 = copy(dve, mask_bf, c["mask"])
    pe.wait(*staged)
    sp.wait(*staged)
    act.wait(*staged)
    m2 = tt(dve, wgate_k, wgate_k, wgate_v, ALU.add)
    m2 = ts(dve, rms_w, rms_w, 1.0, None, ALU.add, None)
    ts(pool, minus_half, const[:, 0:8], 0.0, -0.5, ALU.mult, ALU.add, setup)
    m3 = pool.do(lambda s: nc.gpsimd.memset(ctx1[:, :, :, DX:], 1.0))
    for lane in (pe, act, dve, pool):
        lane.wait(m1, m2, m3)

    def part_a(first):
        if first:
            x_in = x_first
        else:
            x_in = sp.do(lambda s: nc.sync.dma_start(x_tok, x[s].rearrange("(t p) n -> p t n", p=P)), *free["x_tok"], sem=s_x, by=16, apart=True)
        kept = copy(act, x_res, x_tok, x_in, free.get("x_res"))
        x_ready = yield from transposed(x_tok, x_t, x_in, free.get("x_t"))
        free["x_tok"] = (kept, pe.so_far())
        roped = []
        for u in range(2 * QUADS // 2):
            bank, name, bank_free = g_take()
            for m in range(2):
                for k in range(KT):
                    n = (2 * u + m) * P
                    last = mm3(bank[:, m * T:(m + 1) * T], part(wqkv_s, slice(None), k, slice(n, n + P)), part(x_t, slice(None), k),
                               k == 0, k == KT - 1, x_ready, bank_free, mark=k == KT - 1)
            raw, rot, which = qk_raw[u % 2], qk_rot[u % 2], "q" if u < 2 else "k"
            flat = raw.rearrange("p m n -> p (m n)")
            free[name] = r = copy(act, flat, bank, last, free.get(f"qk_raw{u % 2}"), free.get("p_t"), free.get("p_a"))
            cos, sin = (c[w + which].unsqueeze(1).to_broadcast([P, 2, T]) for w in ("cos_", "sin_"))
            s1 = dve.do(lambda s, a=rot, b=raw: nc.vector.stream_shuffle(a.rearrange("p m n -> p (m n)"), b.rearrange("p m n -> p (m n)"), [(i + DA // 2) % DA for i in range(DA)]), r, apart=True)
            s2 = tt(dve, rot, rot, sin, ALU.mult, s1)
            s3 = tt(pool, raw, raw, cos, ALU.mult, r, s1)
            dst = qk[:, 2 * u:2 * u + 2, :]
            roped.append(tt(dve, dst, raw, rot, ALU.add, s2, s3, free.get("qk")))
            free[f"qk_raw{u % 2}"] = roped[-1]
            yield
        for t in range(TT):
            bank, name, bank_free = g_take()
            for k in range(KT):
                last = mm3(bank, part(x_t, slice(None), k, slice(t * P, (t + 1) * P)), part(wqkv_s, slice(None), k, slice(2 * D, 3 * D)),
                           k == 0, k == KT - 1, bank_free, mark=k == KT - 1)
            free[name] = v_ready = copy(act, v_a[:, t, :], bank, last, free.get("v_a"))
            yield
        free["x_t"] = last

        def scores(p):
            i = p % 2
            for t in range(TT):
                for j in range(2):
                    h = 2 * p + j
                    rows = slice(DA * (h % 4), DA * (h % 4) + DA)
                    o = ps_s[:, 2 * i + j, t * P:t * P + P * (t + 1)]
                    mm(o, qk[rows, h // 4, t * P:(t + 1) * P], qk[rows, QUADS + h // 4, 0:P * (t + 1)], t == 0, False,
                       roped[h // 8], roped[2 + h // 8], free.get(f"s{i}"))
            for j in range(2):
                o = ps_s[:, 2 * i + j, :].rearrange("p (a n) -> p a n", a=2)[:, :, 0:P]
                last = mm(o, eye_bf, mask_bf.unsqueeze(1).to_broadcast([P, 2, P]), False, True, mark=True)
            return last

        def softmax(p, scored):
            i = p % 2
            for t in range(TT):
                src = ps_s[:, 2 * i:2 * i + 2, t * P:t * P + P * (t + 1)]
                m = red(neg_max[i][:, :, t], src, ALU.max, scored, free.get(f"neg_max{i}"), negate=True)
            for j in range(2):
                for t in range(TT):
                    e = A(p_a[i][:, j, t * P:t * P + P * (t + 1)], ps_s[:, 2 * i + j, t * P:t * P + P * (t + 1)], ACT.Exp,
                          m, roped[-1], free.get(f"p_a{i}"), bias=neg_max[i][:, j, t:t + 1], accum_out=p_sum[i][:, j, t:t + 1])
            free[f"s{i}"] = free[f"neg_max{i}"] = e
            r = dve.do(lambda s: nc.vector.reciprocal(p_rec[i], p_sum[i]), e)
            for j in range(2):
                for t in range(TT):
                    v = p_a[i][:, j, t * P:t * P + P * (t + 1)]
                    n = ts(pool, v, v, p_rec[i][:, j, t:t + 1], 1.0, ALU.mult, ALU.mult, r)
            return n

        def turn(p, j, ready):
            i = p % 2
            bank, name, bank_free = g_take()
            for n in range(3):
                last = tr(bank[:, n * P:(n + 1) * P], p_a[i][:, j, n * P:(n + 1) * P], eye, ready, bank_free, mark=n == 2)
            if j == 1:
                free[f"p_a{i}"] = free["p_a"] = last
            slot = (2 * p + j) % 4
            lane = dve if j else act
            free[name] = copy(lane, p_t[:, slot, :], bank[:, 0:CAUSAL], last, free.get("p_t"))
            return free[name]

        def attend(q, turned):
            bank, name, bank_free = g_take()
            o = bank[:, 0:T]
            for k in range(TT):
                for j in range(4):
                    h = 4 * q + j
                    strip = slice(DA * j, DA * (j + 1))
                    cols = slice(0, T) if k == 0 else slice(P, T)
                    w = p_t[:, j, 0:T] if k == 0 else p_t[:, j, T:CAUSAL]
                    last = mm(o[strip, cols], v_a[:, k, h * DA:(h + 1) * DA], w, k == 0, k == TT - 1,
                              v_ready, *turned, bank_free, mark=k == TT - 1 and j == 3)
            free["p_t"] = last
            return split(part(att_t, slice(None), q), o, name, last)

        pairs = HA // 2
        ready, turned = [None] * pairs, []
        ready[0] = softmax(0, scores(0))
        yield
        for p in range(pairs):
            if p + 1 < pairs:
                scored = scores(p + 1)
                ready[p + 1] = softmax(p + 1, scored)
                if p + 1 == pairs - 1:
                    free["qk"] = scored
                yield
            for j in range(2):
                turned.append(turn(p, j, ready[p]))
                yield
            if p % 2:
                attended = attend(p // 2, turned)
                turned = []
                yield
        free["v_a"] = pe.so_far()
        ys = []
        for t in range(TT):
            bank, name, bank_free = g_take()
            for k in range(KT):
                last = mm3(bank, part(att_t, slice(None), k, slice(t * P, (t + 1) * P)), part(wout_s, slice(None), k), k == 0, k == KT - 1,
                           attended, bank_free, mark=k == KT - 1)
            free[name] = y = tt(dve, y_a[:, t, :], bank, x_res[:, t, :], ALU.add, last, kept)
            ys.append(y)
            yield
        free["x_t"] = last
        mean, rstd = norm("a", y_a, ys)
        for t in range(TT):
            free["x_res"] = free["lna"] = ts(dve, x1[:, t, :], y_a[:, t, :], ln["a"][1][:, t, 0:1], ln["a"][2][:, t, 0:1], ALU.subtract, ALU.mult,
                                           mean, rstd, free.get("x1_pe"), free.get("x1_dve"))
        done["x1"] = free["x_res"]
        yield

    def part_b():
        ctx_dst = [ctx1[:, t, :, 0:DX] for t in range(TT)]
        for t in range(TT):
            ctx_in = sp.do(lambda s, t=t: nc.sync.dma_start(ctx_dst[t], ctx[s - 1, t * P:(t + 1) * P, :].rearrange("p (h n) -> p h n", h=HX)),
                           free.get("ctx1"), sem=s_ctx, by=16, apart=True)
        x1_in = done["x1"]
        x1_ready = yield from transposed(x1, x1_t, x1_in, free.get("h_raw"))
        free["x1_pe"] = pe.so_far()
        for t in range(TT):
            bank, name, bank_free = g_take()
            for h in range(HX):
                last = tr(bank[:, h * P:(h + 1) * P], ctx1[:, t, h, 0:DX], eye, ctx_in, bank_free, mark=h == HX - 1)
            free[name] = ctx_ready = copy(act, ctx_t[:, :, t * P:(t + 1) * P], bank.rearrange("p (k n) -> p k n", k=KT), last, free.get("y_b"))
            yield
        bank, name, bank_free = g_take()
        for t in range(TT):
            for n, (src, w) in enumerate([(x1_t, wgate_q), (ctx_t, wgate_k)]):
                for k in range(KT):
                    last = mm(bank[:, t * 2 * HX:(t + 1) * 2 * HX], src[:, k, t * P:(t + 1) * P], w[:, k, :], n + k == 0, n == 1 and k == KT - 1,
                              x1_ready, ctx_ready, bank_free, mark=n == 1 and k == KT - 1)
        bias = gate_bias.unsqueeze(1).to_broadcast([P, TT, 2 * HX])
        free[name] = g = tt(dve, gate, bank[:, 0:TT * 2 * HX].rearrange("p (t g) -> p t g", t=TT), bias, ALU.add, last, free.get("gate"))
        yield
        ig, fg = gate[:, :, 0:HX], gate[:, :, HX:]
        m = stt(g_abs, fg, -1.0, fg, ALU.mult, ALU.max, g, free.get("g_abs"))
        m = A(g_exp, g_abs, ACT.Exp, m, scale=-1.0)
        free["g_abs"] = m
        m = A(g_ln, g_exp, ACT.Ln, m, bias=1.0)
        m = stt(log_f, fg, 0.0, g_ln, ALU.min, ALU.subtract, m, free.get("log_f"))
        yield
        bank, name, bank_free = g_take()
        mm(bank[:, 0:HX], upto, log_f[:, 0, :], True, True, m, bank_free)
        mm(bank[:, HX:2 * HX], ones, log_f[:, 0, :], True, False)
        last = mm(bank[:, HX:2 * HX], upto, log_f[:, 1, :], False, True, mark=True)
        free["log_f"] = last
        cs = bank[:, 0:TT * HX].rearrange("p (t h) -> p t h", t=TT)
        m = copy(dve, cum_f, cs, last, free.get("cum_f"))
        free[name] = m
        a_ready = tt(dve, a_col, ig, cum_f, ALU.subtract, m, free.get("a_col"))
        free["gate"] = a_ready
        yield
        bank, name, bank_free = g_take()
        for t in range(TT):
            last = tr(bank[0:HX, t * P:(t + 1) * P], a_col[:, t, :], eye, a_ready, bank_free, mark=t == TT - 1)
        free[name] = m = copy(dve, a_row, bank[0:HX, 0:T], last)
        m_ready = dve.do(lambda s: nc.vector.tensor_tensor_scan(m_row, a_row, a_row, LOWEST, ALU.max, ALU.max), m, free.get("m_row"))
        yield
        for hp in range(HX // 2):
            bank, name, bank_free = g_take()
            for j in range(2):
                last = mm(bank[:, j * T:(j + 1) * T], minus_eye[0:HX, 2 * hp + j:2 * hp + j + 1].to_broadcast([HX, P]), m_row, True, True, m_ready, bank_free, mark=j == 1)
            for j in range(2):
                h = 2 * hp + j
                A(decay[:, h, 0:T], bank[:, j * T:j * T + T], ACT.Exp, last, free.get("c_t"), bias=a_col[:, 0, h:h + 1])
                e = A(decay[:, h, T:CAUSAL], bank[:, j * T + P:j * T + T], ACT.Exp, bias=a_col[:, 1, h:h + 1])
            free[name] = e
            v = decay[:, 2 * hp:2 * hp + 2, 0:P]
            w = decay[:, 2 * hp:2 * hp + 2, T:CAUSAL]
            for block in (v, w):
                d = pool.do(lambda s, b=block: nc.gpsimd.affine_select(out=b, in_=b, compare_op=ALU.is_ge, fill=0.0, base=0,
                                                                       pattern=[[0, 2], [1, P]], channel_multiplier=-1), e, apart=True)
            yield
        free["a_col"] = e
        bank, name, bank_free = g_take()
        for t in range(TT):
            last = tr(bank[:, t * HX:(t + 1) * HX], m_row[:, t * P:(t + 1) * P], eye[0:HX, 0:HX], m_ready, bank_free, mark=t == TT - 1)
        free["m_row"] = last
        free[name] = m = tt(dve, m_col, bank[:, 0:TT * HX].rearrange("p (t h) -> p t h", t=TT), cum_f, ALU.add, last, free.get("em"))
        free["cum_f"] = m
        em_ready = A(em, m_col, ACT.Exp, m, free.get("em"), scale=-1.0)
        cts = []
        for h in range(HX):
            bank, name, bank_free = g_take()
            mm(bank[:, 0:T], ctx_t[:, h, 0:P], x1_t[:, h, :], True, True, bank_free)
            last = mm(bank[:, T:CAUSAL], ctx_t[:, h, P:T], x1_t[:, h, P:T], True, True, mark=True)
            free[name] = m = stt(c_t[:, h, :], bank[:, 0:CAUSAL], float(DX) ** -0.5, decay[:, h, :], ALU.mult, ALU.mult, last, d)
            cts.append(m)
            yield
        turned_used = last
        for t in range(TT):
            for hp in range(HX // 2):
                bank, name, bank_free = g_take()
                for j in range(2):
                    h = 2 * hp + j
                    o = bank[:, j * (DX + 1):(j + 1) * (DX + 1)]
                    for k in range(t + 1):
                        l = c_t[:, h, t * P:(t + 1) * P] if k == 0 else c_t[:, h, T:CAUSAL]
                        last = mm(o, l, ctx1[:, k, h, :], k == 0, k == t, cts[h], bank_free, mark=k == t)
                free[name] = hr = copy(act, h_raw[:, t, 2 * hp:2 * hp + 2, :], bank[:, 0:2 * (DX + 1)].rearrange("p (h n) -> p h n", h=2), last, turned_used)
                yield
        free["c_t"] = free["ctx1"] = last
        hv = h_raw[:, :, :, 0:DX]
        m = tt(dve, h_den, h_raw[:, :, :, DX], em, ALU.max, hr, em_ready)
        free["em"] = m
        m = ts(dve, h_den, h_den, MLSTM_EPS, None, ALU.add, None, m)
        m_den = dve.do(lambda s: nc.vector.reciprocal(h_den, h_den), m)
        for t in range(TT):
            q = A(h_sq[:, t], hv[:, t], ACT.Square, hr, turned_used)
            m = red(h_ssq[:, t], h_sq[:, t], ALU.add, q)
        squared = m
        m = tt(dve, h_ssq, h_ssq, h_den, ALU.mult, m, m_den)
        m = tt(dve, h_ssq, h_ssq, h_den, ALU.mult, m)
        m = ts(dve, h_ssq, h_ssq, 1.0 / DX, RMS_EPS, ALU.mult, ALU.add, m)
        m = tt(pool, h_ssq, h_ssq, minus_half[:, 0:TT * HX].rearrange("p (t h) -> p t h", t=TT), ALU.pow, m)
        m = tt(dve, h_fac, h_ssq, h_den, ALU.mult, m)
        yield
        ys = []
        for t in range(TT):
            m1 = tt(pool, h_sq[:, t], hv[:, t], h_fac[:, t].unsqueeze(2).to_broadcast([P, HX, DX]), ALU.mult, m, squared)
            m2 = tt(dve, h_sq[:, t], h_sq[:, t], rms_w.unsqueeze(1).to_broadcast([P, HX, DX]), ALU.mult, m1)
            ys.append(tt(dve, y_b[:, t, :], h_sq[:, t].rearrange("p h n -> p (h n)"), x1[:, t, :], ALU.add, m2, x1_in))
        free["h_raw"] = m1
        free["x1_dve"] = ys[-1]
        mean, rstd = norm("b", y_b, ys)
        yield
        for t in range(TT):
            free["y_b"] = free["lnb"] = ts(dve, x2[:, t, :], y_b[:, t, :], ln["b"][1][:, t, 0:1], ln["b"][2][:, t, 0:1], ALU.subtract, ALU.mult,
                                           mean, rstd, free.get("x2_pe"), free.get("x2_pool"))
        done["x2"] = free["y_b"]
        yield

    def part_c():
        x2_in = done["x2"]
        x2_ready = yield from transposed(x2, x2_t, x2_in, free.get("x2_t"), x_sum)
        free["x2_pe"] = pe.so_far()
        for t in range(TT):
            with_bo = tt(pool, x2_bo[:, t, :], x2[:, t, :], bo_s, ALU.add, x2_in, free.get("y_c"))
        free["x2_pool"] = with_bo
        bank, name, bank_free = g_take()
        for t in range(TT):
            for k in range(KT):
                last = mm(bank[0:1, 0:HF], x_sum[:, t, k:k + 1], wr_s[:, k, :], t + k == 0, t + k == KT, x2_ready, bank_free, mark=t + k == KT)
        free["x_sum"] = last
        free[name] = m = stt(r_lg, bank[0:1, 0:HF], 1.0 / T, br_s, ALU.mult, ALU.add, last)
        yield
        m = dve.do(lambda s: nc.vector.max(r_top, r_lg), m, apart=True)
        m = ts(dve, r_s[:, 0:1], r_top[:, 0:1], -1.0, None, ALU.mult, None, m)
        m = A(r_e, r_lg, ACT.Exp, m, bias=r_s[:, 0:1], accum_out=r_s[:, 1:2])
        yield
        m = dve.do(lambda s: nc.vector.reciprocal(r_s[:, 2:3], r_s[:, 1:2]), m)
        m = ts(dve, r_dist, r_e, r_s[:, 2:3], None, ALU.mult, None, m)
        m = dve.do(lambda s: nc.vector.max(r_dtop, r_dist), m, apart=True)
        picked = dve.do(lambda s: nc.vector.max_index(r_idx, r_dtop, r_dist), m, apart=True)
        m = ts(dve, r_s[:, 3:4], r_dtop[:, 0:1], -1.0, None, ALU.mult, None, m)
        A(r_eg, r_dtop[:, 0:KF], ACT.Exp, m, bias=r_s[:, 3:4], accum_out=r_s[:, 4:5])
        m = A(r_s[:, 5:6], r_dtop[:, 0:1], ACT.Exp, scale=-1.0)
        for k in range(KF):
            half = slice(DF * (k % 2), DF * (k % 2) + DF)

            def gather(s, k=k, half=half):
                h = nc.vector.value_load(r_idx[0:1, k:k + 1], min_val=0, max_val=HF - 1)
                return nc.vector.tensor_copy(b_sel[half, :, k // 2:k // 2 + 1], bias_col[half, :, bass.ds(h, 1)])
            b_picked = dve.do(gather, picked, free.get("b_sel"), apart=True)
            head = []

            def fetch(s, k=k, j=0, head=head):
                if j == 0:
                    head.append(nc.sync.value_load(r_idx[0:1, k:k + 1], min_val=0, max_val=HF - 1) * DF)
                return nc.sync.dma_start(w_raw[j][:, :, k, :], col((wq, wk, wv)[j])[:, :, bass.ds(head[-1], DF)])
            for j in range(3):
                sp.do(lambda s, j=j, f=fetch: f(s, j=j), picked, *free.get("w_raw", ()), sem=s_w, by=16, apart=True)
            w_in = sp.do(lambda s, k=k, head=head: nc.sync.dma_start(bv_sel[:, k * DF:(k + 1) * DF], bv.unsqueeze(0)[:, bass.ds(head[-1], DF)].to_broadcast([P, DF])),
                         free.get("bv_sel"), sem=s_w, by=16)
        yield
        m = stt(r_s[:, 6:7], r_s[:, 5:6], float(HF - KF), r_s[:, 4:5], ALU.mult, ALU.add, m)
        m = dve.do(lambda s: nc.vector.reciprocal(r_s[:, 7:8], r_s[:, 6:7]), m)
        m = ts(dve, r_g[:, 0:KF], r_eg, r_s[:, 7:8], None, ALU.mult, None, m)
        m = stt(r_g[:, KF:], r_g[:, 0:KF], float(DF) ** -0.5, r_g[:, 0:KF], ALU.mult, ALU.mult, m)
        yield
        bank, name, bank_free = g_take()
        last = mm(bank[:, 0:2 * KF], ones[0:1, :], r_g, True, True, m, bank_free, mark=True)
        free[name] = g_ready = copy(dve, g_bc, bank[:, 0:2 * KF], last, free.get("g_bc"))
        yield
        for j in range(3):
            w_picked = split(part(w_sel, slice(None), slice(None), j), w_raw[j], None, w_in, free.get("w_sel"))
            yield
        for j, dst in enumerate((q_f, k_f)):
            bank, name, bank_free = g_take()
            for m in range(2):
                for k in range(KT):
                    w = [h.rearrange("p h d -> p (h d)") for h in part(w_sel, slice(None), k, j, slice(2 * m, 2 * m + 2))]
                    last = mm3(bank[:, m * T:(m + 1) * T], w, part(x2_t, slice(None), k), k == 0, k == KT - 1, w_picked, bank_free, mark=k == KT - 1)
            for m in range(2):
                qk_ready = ts(dve, dst[:, m, :], bank[:, m * T:(m + 1) * T], b_sel[:, j, m:m + 1], None, ALU.add, None, last, b_picked, free.get("qk_f"))
            free[name] = qk_ready
            yield
        free["b_sel"] = qk_ready
        bank, name, bank_free = g_take()
        for t in range(TT):
            for k in range(KT):
                w = [h.rearrange("p h d -> p (h d)") for h in part(w_sel, slice(None), k, 2)]
                last = mm3(bank[:, t * T:(t + 1) * T], part(x2_t, slice(None), k, slice(t * P, (t + 1) * P)), w, k == 0, k == KT - 1, bank_free, mark=k == KT - 1)
        bv_b = bv_sel.unsqueeze(1).to_broadcast([P, TT, KF * DF])
        v_ready = free[name] = tt(dve, v_f, bank.rearrange("p (t n) -> p t n", t=TT), bv_b, ALU.add, last, w_in, free.get("v_f"))
        free["w_sel"], free["bv_sel"] = last, v_ready
        projected = last
        yield

        def scores(k):
            rows = slice(DF * (k % 2), DF * (k % 2) + DF)
            bank, name, bank_free = g_take()
            for t in range(TT):
                last = mm(bank[:, t * T:(t + 1) * T], q_f[rows, k // 2, t * P:(t + 1) * P], k_f[rows, k // 2, :], True, True, qk_ready, bank_free, mark=t == TT - 1)
            free["qk_f"] = last
            m = red(f_max[:, k, :], bank.rearrange("p (t n) -> p t n", t=TT), ALU.max, last)
            m = ts(dve, f_bias[:, k, :], f_max[:, k, :], g_bc[:, KF + k:KF + k + 1], -1.0, ALU.mult, ALU.mult, m, g_ready, free.get(f"f_bias{k}"))
            for t in range(TT):
                e = A(p_f[k % 2][:, t, :], bank[:, t * T:(t + 1) * T], ACT.Exp, m, w_picked, free.get(f"p_f{k % 2}"), scale=g_bc[:, KF + k:KF + k + 1],
                      bias=f_bias[:, k, t:t + 1], accum_out=f_sum[:, k, t:t + 1])
            free[name] = free[f"f_bias{k}"] = e
            r = dve.do(lambda s: nc.vector.reciprocal(f_rec[:, k, :], f_sum[:, k, :]), e)
            for t in range(TT):
                n = ts(pool, p_f[k % 2][:, t, :], p_f[k % 2][:, t, :], f_rec[:, k, t:t + 1], g_bc[:, k:k + 1], ALU.mult, ALU.mult, r)
            free["g_bc"] = n
            return n

        def turn(k, ready):
            bank, name, bank_free = g_take()
            for kk in range(TT):
                for t in range(TT):
                    last = tr(bank[:, kk * T + t * P:kk * T + (t + 1) * P], p_f[k % 2][:, t, kk * P:(kk + 1) * P], eye, ready, bank_free, mark=t + kk == 2)
            free[f"p_f{k % 2}"] = last
            free[name] = copy(act if k % 2 else dve, pt_f[k % 2].rearrange("p k n -> p (k n)"), bank, last, free.get("pt_f"))
            return free[name]

        ready = [scores(0)]
        yield
        turned = []
        for k in range(KF):
            if k + 1 < KF:
                ready.append(scores(k + 1))
                yield
            turned.append(turn(k, ready[k]))
            yield
            if k % 2:
                bank, name, bank_free = g_take()
                for kk in range(TT):
                    for j in range(2):
                        h = k - 1 + j
                        last = mm(bank[DF * j:DF * (j + 1), 0:T], v_f[:, kk, h * DF:(h + 1) * DF], pt_f[j][:, kk, :], kk == 0, kk == TT - 1,
                                  v_ready, *turned, bank_free, mark=kk + j == 2)
                free["pt_f"] = last
                attended = split(part(att_f, slice(None), k // 2), bank[:, 0:T], name, last, projected)
                turned = []
                yield
        free["v_f"] = last
        ys = []
        for t in range(TT):
            bank, name, bank_free = g_take()
            for k in range(2):
                last = mm3(bank, part(att_f, slice(None), k, slice(t * P, (t + 1) * P)), part(wo_s, slice(None), k), k == 0, k == 1, attended, bank_free, mark=k == 1)
            free[name] = y = tt(dve, y_c[:, t, :], bank, x2_bo[:, t, :], ALU.add, last, with_bo)
            ys.append(y)
            yield
        free["x2_t"] = last
        mean, rstd = norm("c", y_c, ys)
        yield
        _, mv, rs, shift = ln["c"]
        m = stt(shift[:, :, 0], mv[:, :, 0], -1.0, rs[:, :, 0], ALU.mult, ALU.mult, mean, rstd, free.get("y_c"))
        for t in range(TT):
            e = A(y_out[:, t, :], y_c[:, t, :], ACT.Identity, m, w_picked, scale=rs[:, t, 0:1], bias=shift[:, t, 0:1])
        free["y_c"] = free["lnc"] = e
        free["y_out"] = act.do(lambda s: nc.scalar.dma_start(out[s - 2].rearrange("(t p) n -> p t n", p=P), y_out), e, sem=s_out, by=16)
        free["w_raw"] = (free["y_out"], free["p_f0"], free["p_f1"], free["pt_f"])
        yield

    done = {}

    def step(parts, first=False):
        running = {"a": lambda: part_a(first), "b": part_b, "c": part_c}
        running = {n: running[n]() for n in parts}
        g_turn[0] = 0
        for n in ORDER:
            if n in running:
                next(running[n])
        for n in parts:
            assert next(running[n], "end") == "end", "ORDER leaves work undone"

    def end_part():
        for lane in lanes:
            lane.end_part()

    def next_step():
        for lane in lanes:
            lane.step += 1

    LEAD = 3
    TURNS = NB - LEAD
    for parts in ("a", "ab", "abc"):
        step(parts, first=parts == "a")
        next_step()
    end_part()
    before = dict(counts)
    step("abc")
    end_part()
    per_turn = {s: n - before[s] for s, n in counts.items() if n > before[s]}

    def last_turn(m):
        if isinstance(m, tuple):
            return tuple(last_turn(n) for n in m)
        if m is None or m.count <= before.get(m.sem, 0):
            return m
        return Mark(m.sem, m.count + per_turn[m.sem] * (TURNS - 1))
    for marks in (free, done):
        for name, m in marks.items():
            marks[name] = last_turn(m)
    for s, n in per_turn.items():
        counts[s] += n * (TURNS - 1)
    for lane in lanes:
        lane.step += TURNS
    for parts in ("bc", "c"):
        step(parts)
        next_step()
    sp.wait(free["y_out"])
    end_part()

    def program(lane):
        def run(engine):
            lane.run(0, engine)
            with engine.Fori(0, TURNS) as turn:
                lane.run(1, engine, turn, per_turn)
            lane.run(2, engine)
        return run

    with nc.Block() as block:
        block.tensor(program(pe))
        block.scalar(program(act))
        block.vector(program(dve))
        block.gpsimd(program(pool))
        block.sync(program(sp))


INPUTS = ["x", "ctx_1024", "L0_attn_Wqkv", "L0_attn_Wout", "L0_xattn_igate_kernel", "L0_xattn_igate_bias",
          "L0_xattn_fgate_kernel", "L0_xattn_fgate_bias", "L0_xattn_rms_scale", "L0_ffn_Wq", "L0_ffn_bq", "L0_ffn_Wk",
          "L0_ffn_bk", "L0_ffn_Wv", "L0_ffn_bv", "L0_ffn_Wr", "L0_ffn_br", "L0_ffn_Wo", "L0_ffn_bo"]


def kernel(**inputs):
    import concourse.bacc as bacc
    from concourse.bass_utils import run_bass_kernel_spmd

    nc = bacc.Bacc("TRN2", target_bir_lowering=False, num_devices=1)
    arrays, args = {}, []
    for name in INPUTS:
        a = np.ascontiguousarray(inputs[name])
        arrays["in_" + name] = a
        args.append(nc.dram_tensor("in_" + name, a.shape, mybir.dt.from_np(a.dtype), kind="ExternalInput").ap())
    out = nc.dram_tensor("out", (NB, T, D), F32, kind="ExternalOutput").ap()
    build(nc, *args, out)
    r = run_bass_kernel_spmd(nc, [arrays], core_ids=[0])
    return r.results[0]["out"]
```

```python
from concourse import mybir
import concourse.bass as bass
import numpy as np

F32 = mybir.dt.float32
BF16 = mybir.dt.bfloat16
F32R = mybir.dt.float32r
U32 = mybir.dt.uint32
ALU = mybir.AluOpType
ACT = mybir.ActivationFunctionType
AX = mybir.AxisListType

P = 128
NB, T, D = 32, 256, 512
TT, KT = T // P, D // P
HA, DA = 16, D // 16
QUADS = HA // 4
HX = 4
DX = D // HX
HF, KF, DF = 16, 4, 64
CAUSAL = P + T
LN_EPS, MLSTM_EPS, RMS_EPS = 1e-5, 1e-6, 1e-6
MASKED = -1e30
LOWEST = -3e38
ORDER = (
    "bbbbccccababaacbccbacacaabaabbaaaaaaacacbabcacacaaababaaaaabcaabcbabcaaabaaaaaccaaaababaaccaacaccaab"
    "abcaabbaaacbbcaaacbaccccbcabcaaccaababbcaaaabacbcbbaaaababacbacccbabaaccaacabcaaacaaaaacbcabacaabaca"
    "bcaaaaa"
)


class Mark:

    def __init__(self, sem, count):
        self.sem, self.count = sem, count


class Lane:

    def __init__(self, nc, name, counts):
        self.sem, self.counts = nc.alloc_semaphore(name + "_done"), counts
        self.spare = nc.alloc_semaphore(name + "_spare")
        self.part, self.parts, self.seen, self.step = [], [], {}, 0

    def wait(self, *marks):
        for m in marks:
            if m is not None and self.seen.get(m.sem, -1) < m.count:
                self.seen[m.sem] = m.count
                self.part.append((None, m, 0, self.step))

    def do(self, make, *after, mark=True, sem=None, by=1, apart=False):
        for m in after:
            queued = len(self.part)
            self.wait(m)
            if apart and len(self.part) > queued:
                self.part.append((None, None, 0, self.step))
        sem = sem or (self.sem if mark else None)
        self.part.append((make, sem, by, self.step))
        if sem is None:
            return None
        self.counts[sem] = self.counts.get(sem, 0) + by
        return Mark(sem, self.counts[sem])

    def so_far(self):
        return Mark(self.sem, self.counts[self.sem])

    def end_part(self):
        self.parts.append(self.part)
        self.part, self.seen = [], {}

    def run(self, part, engine, turn=None, per_turn=None):
        for make, what, by, step in self.parts[part]:
            if make is None and what is None:
                if turn is not None:
                    engine.sem_inc(self.spare, 1)
            elif make is None:
                engine.wait_ge(what.sem, what.count if turn is None or what.sem not in per_turn else turn * per_turn[what.sem] + what.count)
            else:
                made = make(step if turn is None else turn + step)
                if what is not None:
                    made.then_inc(what, by)


def constants():
    half = DA // 2
    theta = (1.0 / 10000.0 ** (np.arange(half, dtype=np.float32) / np.float32(half))).astype(np.float32)
    freqs = (theta[:, None] * np.arange(T, dtype=np.float32)[None, :]).astype(np.float32)
    cos = np.tile(np.cos(freqs), (2 * P // DA, 1))
    sin = np.tile(np.concatenate([-np.sin(freqs), np.sin(freqs)]), (P // DA, 1))
    root = np.float32(1.0 / np.sqrt(DA))
    eye = np.eye(P, dtype=np.float32)
    upto = np.triu(np.ones((P, P), np.float32))
    parts = {"cos_q": cos * root, "sin_q": sin * root, "cos_k": cos, "sin_k": sin, "eye": eye,
             "upto": upto, "minus_eye": -eye[:, 0:HX], "ones": np.ones((P, P), np.float32),
             "mask": np.where(upto.T > 0, 0.0, MASKED)}
    where, at = {}, 0
    for name, a in parts.items():
        where[name] = (at, at + a.shape[1])
        at += a.shape[1]
    return np.concatenate([a.astype(np.float32) for a in parts.values()], axis=1), where


def build(nc, x, ctx, wqkv, wout, igk, igb, fgk, fgb, rms, wq, bq, wk, bk, wv, bv, wr, br, wo, bo, out):
    counts = {}
    pe, act, dve, pool, sp = lanes = [Lane(nc, n, counts) for n in ("pe", "act", "dve", "pool", "sp")]
    s_setup, s_x, s_ctx, s_out, *s_w = (nc.alloc_semaphore(n) for n in ("setup_loaded", "x_loaded", "ctx_loaded", "out_stored", "wq_picked", "wk_picked", "wv_picked", *(f"staged{i}" for i in range(6))))
    s_w, s_stage = s_w[:3], s_w[3:]

    def sb(name, shape, dt=F32):
        return nc.alloc_sbuf_tensor(name, shape, dt).ap()

    table, where = constants()
    const = sb("const", [P, table.shape[1]])
    c = {n: const[:, a:b] for n, (a, b) in where.items()}
    eye, ones, upto = c["eye"], c["ones"], c["upto"]
    minus_eye = c["minus_eye"]
    eye_bf = sb("eye_bf", [P, P], BF16)
    mask_bf = sb("mask_bf", [P, P], BF16)

    def halves(name, shape):
        return [sb(f"{name}_{part}", shape, F32R) for part in ("hi", "lo")]

    wqkv_s = halves("wqkv", [P, KT, 3 * D])
    wout_s = halves("wout", [P, KT, D])
    wgate_q = sb("wgate_q", [P, KT, 2 * HX])
    wgate_k = sb("wgate_k", [P, KT, 2 * HX])
    wgate_v = sb("wgate_v", [P, KT, 2 * HX])
    gate_bias = sb("gate_bias", [P, 2 * HX])
    rms_w = sb("rms_w", [P, DX])
    bias_col = sb("bias_col", [P, 3, HF])
    wr_s = sb("wr_s", [P, KT, HF])
    br_s = sb("br_s", [1, HF])
    wo_s = halves("wo", [P, KF * DF // P, D])
    bo_s = sb("bo_s", [P, D])
    minus_half = sb("minus_half", [P, 8])

    x_tok = sb("x_tok", [P, TT, D])
    x_res = sb("x_res", [P, TT, D])
    x_t = halves("x_t", [P, KT, T])
    qk = sb("qk", [P, 2 * QUADS, T])
    v_a = sb("v_a", [P, TT, D])
    neg_max = [sb(f"neg_max{i}", [P, 2, TT]) for i in range(2)]
    p_sum = [sb(f"p_sum{i}", [P, 2, TT]) for i in range(2)]
    p_rec = [sb(f"p_rec{i}", [P, 2, TT]) for i in range(2)]
    p_a = [sb(f"p_a{i}", [P, 2, CAUSAL]) for i in range(2)]
    p_t = sb("p_t", [P, 4, CAUSAL])
    qk_raw = [p_t.rearrange("p h n -> p (h n)")[:, i * 2 * T:(i + 1) * 2 * T].rearrange("p (m n) -> p m n", m=2) for i in range(2)]
    qk_rot = [p_a[i].rearrange("p h n -> p (h n)")[:, 0:2 * T].rearrange("p (m n) -> p m n", m=2) for i in range(2)]
    att_t = x_t
    y_a = x_res
    x1 = sb("x1", [P, TT, D])
    ctx1 = sb("ctx1", [P, TT, HX, DX + 1])
    h_raw = sb("h_raw", [P, TT, HX, DX + 1])
    x1_t = h_raw.rearrange("p t h n -> p (t h n)")[:, 0:KT * T].rearrange("p (k n) -> p k n", k=KT)
    ctx_t = sb("ctx_t", [P, KT, T])
    gate = sb("gate", [P, TT, 2 * HX])
    g_abs, g_exp, g_ln, log_f, cum_f, a_col, m_col, em = (sb(n, [P, TT, HX]) for n in ("g_abs", "g_exp", "g_ln", "log_f", "cum_f", "a_col", "m_col", "em"))
    a_row = sb("a_row", [HX, T])
    m_row = sb("m_row", [HX, T])
    decay = sb("decay", [P, HX, CAUSAL])
    c_t = decay
    h_sq = ctx_t.rearrange("p k (t n) -> p (k t n)", t=TT).rearrange("p (t h n) -> p t h n", t=TT, h=HX)
    h_ssq, h_den, h_fac = (sb(n, [P, TT, HX]) for n in ("h_ssq", "h_den", "h_fac"))
    y_b = h_sq.rearrange("p t h n -> p t (h n)")
    x2 = sb("x2", [P, TT, D])
    x2_t = halves("x2_t", [P, KT, T])
    x_sum = sb("x_sum", [P, TT, KT])
    r_lg, r_e, r_dist = (sb(n, [1, HF]) for n in ("r_lg", "r_e", "r_dist"))
    r_top, r_dtop = (sb(n, [1, 8]) for n in ("r_top", "r_dtop"))
    r_idx = sb("r_idx", [1, 8], U32)
    r_s = sb("r_s", [1, 8])
    r_eg = sb("r_eg", [1, KF])
    r_g = sb("r_g", [1, 2 * KF])
    g_bc = sb("g_bc", [P, 2 * KF])
    w_sel = halves("w_sel", [P, KT, 3, KF, DF])
    b_sel = sb("b_sel", [P, 3, KF // 2])
    b_v = sb("b_v", [P, KF // 2])
    q_f = sb("q_f", [P, 2, T])
    k_f = sb("k_f", [P, 2, T])
    v_f = sb("v_f", [P, TT, KF * DF])
    f_max = sb("f_max", [P, KF, TT])
    f_bias = sb("f_bias", [P, KF, TT])
    f_sum = sb("f_sum", [P, KF, TT])
    f_rec = sb("f_rec", [P, KF, TT])
    p_all = sb("p_all", [P, 2, TT, T])
    pt_all = sb("pt_all", [P, 2, TT, T])
    p_f = [p_all[:, i] for i in range(2)]
    pt_f = [pt_all[:, i] for i in range(2)]
    att_f = [h[:, 0:2, :] for h in x2_t]
    x2_bo = sb("x2_bo", [P, TT, D])
    y_c = x2_bo
    y_out = sb("y_out", [P, TT, D])
    w_raw = [p_all.rearrange("p i t n -> p (i t n)"), pt_all.rearrange("p i t n -> p (i t n)"), y_out.rearrange("p t n -> p (t n)")]
    w_raw = [w.rearrange("p (k h d) -> p k h d", k=KT, h=KF) for w in w_raw]
    ln = {s: [sb(f"ln_{n}_{s}", [P, TT, w]) for n, w in (("stat", 6), ("mv", 2), ("rstd", 1), ("shift", 1))] for s in "abc"}

    ps_s = nc.alloc_psum_tensor("ps_s", [P, 4, D], F32).ap()
    RING = 4
    ps_g = [nc.alloc_psum_tensor(f"ps_g{i}", [P, D], F32).ap() for i in range(RING)]
    free = {}
    idle, in_use = [], []

    def g_take():
        for i in [i for i in in_use if free[f"g{i}"] is not None]:
            in_use.remove(i)
            idle.append(i)
        assert idle, "ORDER takes a bank that is still in use"
        i = idle.pop(0)
        in_use.append(i)
        released, free[f"g{i}"] = free.get(f"g{i}"), None
        return ps_g[i], f"g{i}", released

    def mm(o, l, r, start, stop, *after, mark=False):
        return pe.do(lambda s: nc.tensor.matmul(o, l, r, start=start, stop=stop), *after, mark=mark)

    def mm3(o, l, r, first, last, *after, mark=False):
        mm(o, l[0], r[0], first, False, *after)
        mm(o, l[0], r[1], False, False)
        return mm(o, l[1], r[0], False, last, mark=mark)

    def part(pair, *at):
        return [h[at] for h in pair]

    def split(dst, src, bank, *after):
        a = copy(act, dst[0], src, *after)
        m = tt(dve, dst[1], src, dst[0].bitcast(F32), ALU.subtract, a)
        if bank:
            free[bank] = m
        return m

    def tr(o, i, ident, *after, mark=False):
        return pe.do(lambda s: nc.tensor.transpose(o, i, ident), *after, mark=mark, apart=i.shape[0] < P)

    def A(o, i, f, *after, **kw):
        return act.do(lambda s: nc.scalar.activation(o, i, f, **kw), *after)

    def tt(lane, o, a, b, op, *after):
        e = nc.vector if lane is dve else nc.gpsimd
        return lane.do(lambda s: e.tensor_tensor(o, a, b, op), *after)

    def ts(lane, o, a, s1, s2, op0, op1, *after):
        e = nc.vector if lane is dve else nc.gpsimd
        apart = lane is pool
        if op1 is None:
            return lane.do(lambda s: e.tensor_scalar(o, a, s1, None, op0), *after, apart=apart)
        return lane.do(lambda s: e.tensor_scalar(o, a, s1, s2, op0, op1), *after, apart=apart)

    def stt(o, a, sc, b, op0, op1, *after):
        return dve.do(lambda s: nc.vector.scalar_tensor_tensor(o, a, sc, b, op0, op1), *after)

    def red(o, a, op, *after, negate=False):
        return dve.do(lambda s: nc.vector.tensor_reduce(o, a, AX.X, op, negate=negate), *after)

    def copy(lane, o, a, *after):
        if lane is act:
            return act.do(lambda s: nc.scalar.copy(o, a), *after)
        e = nc.vector if lane is dve else nc.gpsimd
        return lane.do(lambda s: e.tensor_copy(o, a), *after)

    def transposed(src, dst, ready, dst_free, sums=None):
        m = []
        for t in range(TT):
            bank, name, bank_free = g_take()
            for k in range(KT):
                last = tr(bank[:, k * P:(k + 1) * P], src[:, t, k * P:(k + 1) * P], eye, ready, bank_free, mark=k == KT - 1)
            yield
            blocks = bank.rearrange("p (k n) -> p k n", k=KT)
            if isinstance(dst, list):
                m.append(split(part(dst, slice(None), slice(None), slice(t * P, (t + 1) * P)), blocks, name, last, dst_free))
            else:
                m.append(copy(act, dst[:, :, t * P:(t + 1) * P], blocks, last, dst_free))
            if sums is not None:
                m[-1] = red(sums[:, t, :], blocks, ALU.add, m[-1], free.get("x_sum"))
            free[name] = m[-1]
            yield
        return m[-1]

    def norm(which, y, ready):
        stat, mv, rstd, _ = ln[which]
        for t in range(TT):
            m = dve.do(lambda s, t=t: nc.vector.bn_stats(stat[:, t, :], y[:, t, :]), ready[t], free.get("ln" + which))
        for t in range(TT):
            m = dve.do(lambda s, t=t: nc.vector.bn_aggr(mv[:, t, :], stat[:, t, :]), m, apart=True)
        e = ts(pool, rstd[:, :, 0], mv[:, :, 1], LN_EPS, None, ALU.add, None, m, free.get("ln" + which))
        return m, tt(pool, rstd[:, :, 0], rstd[:, :, 0], minus_half[:, 0:TT], ALU.pow, e)

    loads = []

    def load(dst, src, odd=False):
        def make(s):
            if odd:
                with nc.allow_non_contiguous_dma(reason="a few short columns, once"):
                    return nc.sync.dma_start(dst, src)
            return nc.sync.dma_start(dst, src)
        loads.append(sp.do(make, sem=s_setup, by=16))

    col = lambda w: w.rearrange("(k p) n -> p k n", p=P)
    row = lambda b, n: b.unsqueeze(0).to_broadcast([P, n])
    sp.do(lambda s: nc.sync.dma_start(x_tok, x[0].rearrange("(t p) n -> p t n", p=P)), sem=s_x, by=16)
    done = {"x": Mark(s_x, 16)}
    load(const, nc.inline_tensor(table, name="tables").ap())
    for i, w in enumerate((wgate_q, wgate_k, wgate_v)):
        for j, g in enumerate((igk, fgk)):
            load(w[:, :, j * HX:(j + 1) * HX], col(g[i * D:(i + 1) * D, :]), odd=True)
    load(gate_bias[:, 0:HX], row(igb, HX))
    load(gate_bias[:, HX:], row(fgb, HX))
    load(rms_w, row(rms, DX))
    for j, b in enumerate((bq, bk, bv)):
        for half in range(2):
            load(bias_col[half * DF:(half + 1) * DF, j, :], b.rearrange("(h d) -> d h", d=DF), odd=True)
    load(wr_s, col(wr))
    load(br_s, br.unsqueeze(0))
    load(bo_s, row(bo, D))
    setup = loads[-1]
    stages = [p_all.rearrange("p i t n -> p (i t n)"), pt_all.rearrange("p i t n -> p (i t n)"), y_out.rearrange("p t n -> p (t n)"),
              x2_bo.rearrange("p t n -> p (t n)"), x2.rearrange("p t n -> p (t n)"), x1.rearrange("p t n -> p (t n)")]
    pieces = [(col(wqkv)[:, 2 * k:2 * k + 2, j * D:(j + 1) * D], part(wqkv_s, slice(None), slice(2 * k, 2 * k + 2), slice(j * D, (j + 1) * D))) for j in range(3) for k in range(2)]
    pieces += [(col(wout)[:, 2 * k:2 * k + 2, :], part(wout_s, slice(None), slice(2 * k, 2 * k + 2), slice(None))) for k in range(2)]
    pieces += [(col(wo), wo_s)]
    stage_free = [None] * len(stages)
    staged = []
    for n, (src, dst) in enumerate(pieces):
        i = n % len(stages)
        buf = stages[i].rearrange("p (k n) -> p k n", k=2)
        m = sp.do(lambda s, b=buf, src=src: nc.sync.dma_start(b, src), stage_free[i], sem=s_stage[i], by=16)
        stage_free[i] = split(dst, buf, None, m)
        staged.append(stage_free[i])
    for lane in (pe, act):
        lane.wait(setup)
    copy(dve, eye_bf, eye, setup)
    m1 = copy(dve, mask_bf, c["mask"])
    pe.wait(*staged)
    sp.wait(*staged)
    act.wait(*staged)
    m2 = tt(dve, wgate_k, wgate_k, wgate_v, ALU.add)
    m2 = ts(dve, rms_w, rms_w, 1.0, None, ALU.add, None)
    ts(pool, minus_half, const[:, 0:8], 0.0, -0.5, ALU.mult, ALU.add, setup)
    m3 = pool.do(lambda s: nc.gpsimd.memset(ctx1[:, :, :, DX:], 1.0))
    for lane in (pe, act, dve, pool):
        lane.wait(m1, m2, m3)

    def part_a(last_one):
        x_in = done["x"]
        kept = copy(act, x_res, x_tok, x_in, free.get("x_res"))
        x_ready = yield from transposed(x_tok, x_t, x_in, free.get("x_t"))
        if not last_one:
            done["x"] = sp.do(lambda s: nc.sync.dma_start(x_tok, x[s + 1].rearrange("(t p) n -> p t n", p=P)), kept, pe.so_far(), sem=s_x, by=16, apart=True)
        roped = []
        for u in range(2 * QUADS // 2):
            bank, name, bank_free = g_take()
            for m in range(2):
                for k in range(KT):
                    n = (2 * u + m) * P
                    last = mm3(bank[:, m * T:(m + 1) * T], part(wqkv_s, slice(None), k, slice(n, n + P)), part(x_t, slice(None), k),
                               k == 0, k == KT - 1, x_ready, bank_free, mark=k == KT - 1)
                yield
            raw, rot, which = qk_raw[u % 2], qk_rot[u % 2], "q" if u < 2 else "k"
            flat = raw.rearrange("p m n -> p (m n)")
            free[name] = r = copy(act, flat, bank, last, free.get(f"qk_raw{u % 2}"), free.get("p_t"), free.get("p_a"))
            cos, sin = (c[w + which].unsqueeze(1).to_broadcast([P, 2, T]) for w in ("cos_", "sin_"))
            s1 = dve.do(lambda s, a=rot, b=raw: nc.vector.stream_shuffle(a.rearrange("p m n -> p (m n)"), b.rearrange("p m n -> p (m n)"), [(i + DA // 2) % DA for i in range(DA)]), r, apart=True)
            s3 = tt(pool, raw, raw, cos, ALU.mult, r, s1)
            s2 = tt(dve, rot, rot, sin, ALU.mult, s1)
            yield
            dst = qk[:, 2 * u:2 * u + 2, :]
            roped.append(tt(dve, dst, raw, rot, ALU.add, s2, s3, free.get("qk")))
            free[f"qk_raw{u % 2}"] = roped[-1]
            yield
        for t in range(TT):
            bank, name, bank_free = g_take()
            for k in range(KT):
                last = mm3(bank, part(x_t, slice(None), k, slice(t * P, (t + 1) * P)), part(wqkv_s, slice(None), k, slice(2 * D, 3 * D)),
                           k == 0, k == KT - 1, bank_free, mark=k == KT - 1)
                if k % 2:
                    yield
            free[name] = v_ready = copy(act, v_a[:, t, :], bank, last, free.get("v_a"))
            yield
        free["x_t"] = last

        def scores(p):
            i = p % 2
            for t in range(TT):
                for j in range(2):
                    h = 2 * p + j
                    rows = slice(DA * (h % 4), DA * (h % 4) + DA)
                    o = ps_s[:, 2 * i + j, t * P:t * P + P * (t + 1)]
                    mm(o, qk[rows, h // 4, t * P:(t + 1) * P], qk[rows, QUADS + h // 4, 0:P * (t + 1)], t == 0, False,
                       roped[h // 8], roped[2 + h // 8], free.get(f"s{i}"))
            for j in range(2):
                o = ps_s[:, 2 * i + j, :].rearrange("p (a n) -> p a n", a=2)[:, :, 0:P]
                last = mm(o, eye_bf, mask_bf.unsqueeze(1).to_broadcast([P, 2, P]), False, True, mark=True)
            return last

        def exps(p, scored):
            i = p % 2
            for t in range(TT):
                src = ps_s[:, 2 * i:2 * i + 2, t * P:t * P + P * (t + 1)]
                m = red(neg_max[i][:, :, t], src, ALU.max, scored, free.get(f"neg_max{i}"), negate=True)
            yield
            for j in range(2):
                for t in range(TT):
                    e = A(p_a[i][:, j, t * P:t * P + P * (t + 1)], ps_s[:, 2 * i + j, t * P:t * P + P * (t + 1)], ACT.Exp,
                          m, roped[-1], free.get(f"p_a{i}"), bias=neg_max[i][:, j, t:t + 1], accum_out=p_sum[i][:, j, t:t + 1])
            free[f"s{i}"] = free[f"neg_max{i}"] = e
            return e

        def normalise(p, summed):
            i = p % 2
            r = dve.do(lambda s: nc.vector.reciprocal(p_rec[i], p_sum[i]), summed)
            n = []
            for t, lane in ((0, pool), (1, dve)):
                for j in range(2):
                    v = p_a[i][:, j, t * P:t * P + P * (t + 1)]
                    n.append(ts(lane, v, v, p_rec[i][:, j, t:t + 1], 1.0, ALU.mult, ALU.mult, r))
            return n

        def turn(p, j, ready):
            i = p % 2
            bank, name, bank_free = g_take()
            for n in range(3):
                last = tr(bank[:, n * P:(n + 1) * P], p_a[i][:, j, n * P:(n + 1) * P], eye, *ready, bank_free, mark=n == 2)
            if j == 1:
                free[f"p_a{i}"] = free["p_a"] = last
            yield
            slot = (2 * p + j) % 4
            lane = dve if j else act
            free[name] = copy(lane, p_t[:, slot, :], bank[:, 0:CAUSAL], last, free.get("p_t"))
            return free[name]

        def attend(q, turned):
            bank, name, bank_free = g_take()
            o = bank[:, 0:T]
            for k in range(TT):
                for j in range(4):
                    h = 4 * q + j
                    strip = slice(DA * j, DA * (j + 1))
                    cols = slice(0, T) if k == 0 else slice(P, T)
                    w = p_t[:, j, 0:T] if k == 0 else p_t[:, j, T:CAUSAL]
                    last = mm(o[strip, cols], v_a[:, k, h * DA:(h + 1) * DA], w, k == 0, k == TT - 1,
                              v_ready, *turned, bank_free, mark=k == TT - 1 and j == 3)
            free["p_t"] = last
            yield
            return split(part(att_t, slice(None), q), o, name, last)

        pairs = HA // 2
        turned = []
        scored = scores(0)
        yield
        summed = yield from exps(0, scored)
        yield
        for p in range(pairs):
            if p + 1 < pairs:
                scored = scores(p + 1)
                if p + 1 == pairs - 1:
                    free["qk"] = scored
                yield
                next_summed = yield from exps(p + 1, scored)
                yield
            ready = normalise(p, summed)
            summed = next_summed
            yield
            for j in range(2):
                turned.append((yield from turn(p, j, ready)))
                yield
            if p % 2:
                attended = yield from attend(p // 2, turned)
                turned = []
                yield
        free["v_a"] = pe.so_far()
        ys = []
        for t in range(TT):
            bank, name, bank_free = g_take()
            for k in range(KT):
                last = mm3(bank, part(att_t, slice(None), k, slice(t * P, (t + 1) * P)), part(wout_s, slice(None), k), k == 0, k == KT - 1,
                           attended, bank_free, mark=k == KT - 1)
                if k % 2:
                    yield
            free[name] = y = tt(dve, y_a[:, t, :], bank, x_res[:, t, :], ALU.add, last, kept)
            ys.append(y)
            yield
        free["x_t"] = last
        mean, rstd = norm("a", y_a, ys)
        yield
        for t in range(TT):
            done["ctx"] = sp.do(lambda s, t=t: nc.sync.dma_start(ctx1[:, t, :, 0:DX], ctx[s, t * P:(t + 1) * P, :].rearrange("p (h n) -> p h n", h=HX)),
                                free.get("ctx1"), sem=s_ctx, by=16, apart=True)
        for t in range(TT):
            free["x_res"] = free["lna"] = ts(dve, x1[:, t, :], y_a[:, t, :], ln["a"][1][:, t, 0:1], ln["a"][2][:, t, 0:1], ALU.subtract, ALU.mult,
                                           mean, rstd, free.get("x1_pe"), free.get("x1_dve"))
        done["x1"] = free["x_res"]
        yield

    def part_b():
        ctx_in = done["ctx"]
        for t in range(TT):
            bank, name, bank_free = g_take()
            for h in range(HX):
                last = tr(bank[:, h * P:(h + 1) * P], ctx1[:, t, h, 0:DX], eye, ctx_in, bank_free, mark=h == HX - 1)
            yield
            free[name] = ctx_ready = copy(act, ctx_t[:, :, t * P:(t + 1) * P], bank.rearrange("p (k n) -> p k n", k=KT), last, free.get("y_b"))
            yield
        x1_in = done["x1"]
        x1_ready = yield from transposed(x1, x1_t, x1_in, free.get("h_raw"))
        free["x1_pe"] = pe.so_far()
        bank, name, bank_free = g_take()
        for t in range(TT):
            for n, (src, w) in enumerate([(x1_t, wgate_q), (ctx_t, wgate_k)]):
                for k in range(KT):
                    last = mm(bank[:, t * 2 * HX:(t + 1) * 2 * HX], src[:, k, t * P:(t + 1) * P], w[:, k, :], n + k == 0, n == 1 and k == KT - 1,
                              x1_ready, ctx_ready, bank_free, mark=n == 1 and k == KT - 1)
        yield
        bias = gate_bias.unsqueeze(1).to_broadcast([P, TT, 2 * HX])
        free[name] = g = tt(dve, gate, bank[:, 0:TT * 2 * HX].rearrange("p (t g) -> p t g", t=TT), bias, ALU.add, last, free.get("gate"))
        yield
        ig, fg = gate[:, :, 0:HX], gate[:, :, HX:]
        m = stt(g_abs, fg, -1.0, fg, ALU.mult, ALU.max, g, free.get("g_abs"))
        yield
        m = A(g_exp, g_abs, ACT.Exp, m, scale=-1.0)
        free["g_abs"] = m
        m = A(g_ln, g_exp, ACT.Ln, m, bias=1.0)
        yield
        m = stt(log_f, fg, 0.0, g_ln, ALU.min, ALU.subtract, m, free.get("log_f"))
        yield
        bank, name, bank_free = g_take()
        mm(bank[:, 0:HX], upto, log_f[:, 0, :], True, True, m, bank_free)
        mm(bank[:, HX:2 * HX], ones, log_f[:, 0, :], True, False)
        last = mm(bank[:, HX:2 * HX], upto, log_f[:, 1, :], False, True, mark=True)
        free["log_f"] = last
        yield
        cs = bank[:, 0:TT * HX].rearrange("p (t h) -> p t h", t=TT)
        m = copy(dve, cum_f, cs, last, free.get("cum_f"))
        free[name] = m
        a_ready = tt(dve, a_col, ig, cum_f, ALU.subtract, m, free.get("a_col"))
        free["gate"] = a_ready
        yield
        bank, name, bank_free = g_take()
        for t in range(TT):
            last = tr(bank[0:HX, t * P:(t + 1) * P], a_col[:, t, :], eye, a_ready, bank_free, mark=t == TT - 1)
        yield
        free[name] = m = copy(dve, a_row, bank[0:HX, 0:T], last)
        m_ready = dve.do(lambda s: nc.vector.tensor_tensor_scan(m_row, a_row, a_row, LOWEST, ALU.max, ALU.max), m, free.get("m_row"))
        yield
        for hp in range(HX // 2):
            bank, name, bank_free = g_take()
            for j in range(2):
                last = mm(bank[:, j * T:(j + 1) * T], minus_eye[0:HX, 2 * hp + j:2 * hp + j + 1].to_broadcast([HX, P]), m_row, True, True, m_ready, bank_free, mark=j == 1)
            yield
            for j in range(2):
                h = 2 * hp + j
                A(decay[:, h, 0:T], bank[:, j * T:j * T + T], ACT.Exp, last, free.get("c_t"), bias=a_col[:, 0, h:h + 1])
                e = A(decay[:, h, T:CAUSAL], bank[:, j * T + P:j * T + T], ACT.Exp, bias=a_col[:, 1, h:h + 1])
            free[name] = e
            yield
            v = decay[:, 2 * hp:2 * hp + 2, 0:P]
            w = decay[:, 2 * hp:2 * hp + 2, T:CAUSAL]
            for block in (v, w):
                d = pool.do(lambda s, b=block: nc.gpsimd.affine_select(out=b, in_=b, compare_op=ALU.is_ge, fill=0.0, base=0,
                                                                       pattern=[[0, 2], [1, P]], channel_multiplier=-1), e, apart=True)
            yield
        free["a_col"] = e
        bank, name, bank_free = g_take()
        for t in range(TT):
            last = tr(bank[:, t * HX:(t + 1) * HX], m_row[:, t * P:(t + 1) * P], eye[0:HX, 0:HX], m_ready, bank_free, mark=t == TT - 1)
        free["m_row"] = last
        yield
        free[name] = m = tt(dve, m_col, bank[:, 0:TT * HX].rearrange("p (t h) -> p t h", t=TT), cum_f, ALU.add, last, free.get("em"))
        free["cum_f"] = m
        yield
        em_ready = A(em, m_col, ACT.Exp, m, free.get("em"), scale=-1.0)
        cts = []
        for h in range(HX):
            bank, name, bank_free = g_take()
            mm(bank[:, 0:T], ctx_t[:, h, 0:P], x1_t[:, h, :], True, True, bank_free)
            last = mm(bank[:, T:CAUSAL], ctx_t[:, h, P:T], x1_t[:, h, P:T], True, True, mark=True)
            yield
            free[name] = m = stt(c_t[:, h, :], bank[:, 0:CAUSAL], float(DX) ** -0.5, decay[:, h, :], ALU.mult, ALU.mult, last, d)
            cts.append(m)
            yield
        turned_used = last
        for t in range(TT):
            for hp in range(HX // 2):
                bank, name, bank_free = g_take()
                for j in range(2):
                    h = 2 * hp + j
                    o = bank[:, j * (DX + 1):(j + 1) * (DX + 1)]
                    for k in range(t + 1):
                        l = c_t[:, h, t * P:(t + 1) * P] if k == 0 else c_t[:, h, T:CAUSAL]
                        last = mm(o, l, ctx1[:, k, h, :], k == 0, k == t, cts[h], bank_free, mark=k == t)
                yield
                free[name] = hr = copy(act, h_raw[:, t, 2 * hp:2 * hp + 2, :], bank[:, 0:2 * (DX + 1)].rearrange("p (h n) -> p h n", h=2), last, turned_used)
                yield
        free["c_t"] = free["ctx1"] = last
        hv = h_raw[:, :, :, 0:DX]
        m = tt(dve, h_den, h_raw[:, :, :, DX], em, ALU.max, hr, em_ready)
        free["em"] = m
        m = ts(dve, h_den, h_den, MLSTM_EPS, None, ALU.add, None, m)
        m_den = dve.do(lambda s: nc.vector.reciprocal(h_den, h_den), m)
        q = [A(h_sq[:, t], hv[:, t], ACT.Square, hr, turned_used) for t in range(TT)]
        yield
        for t in range(TT):
            m = red(h_ssq[:, t], h_sq[:, t], ALU.add, q[t])
        squared = m
        m = tt(dve, h_ssq, h_ssq, h_den, ALU.mult, m, m_den)
        m = tt(dve, h_ssq, h_ssq, h_den, ALU.mult, m)
        m = ts(dve, h_ssq, h_ssq, 1.0 / DX, RMS_EPS, ALU.mult, ALU.add, m)
        m = tt(pool, h_ssq, h_ssq, minus_half[:, 0:TT * HX].rearrange("p (t h) -> p t h", t=TT), ALU.pow, m)
        yield
        m = tt(dve, h_fac, h_ssq, h_den, ALU.mult, m)
        yield
        ys = []
        m1s = [tt(pool, h_sq[:, t], hv[:, t], h_fac[:, t].unsqueeze(2).to_broadcast([P, HX, DX]), ALU.mult, m, squared) for t in range(TT)]
        for t in range(TT):
            yield
            m1 = m1s[t]
            m2 = tt(dve, h_sq[:, t], h_sq[:, t], rms_w.unsqueeze(1).to_broadcast([P, HX, DX]), ALU.mult, m1)
            ys.append(tt(dve, y_b[:, t, :], h_sq[:, t].rearrange("p h n -> p (h n)"), x1[:, t, :], ALU.add, m2, x1_in))
        free["h_raw"] = m1
        free["x1_dve"] = ys[-1]
        mean, rstd = norm("b", y_b, ys)
        yield
        for t in range(TT):
            free["y_b"] = free["lnb"] = ts(dve, x2[:, t, :], y_b[:, t, :], ln["b"][1][:, t, 0:1], ln["b"][2][:, t, 0:1], ALU.subtract, ALU.mult,
                                           mean, rstd, free.get("x2_pe"), free.get("x2_pool"))
        done["x2"] = free["y_b"]
        yield

    def part_c():
        x2_in = done["x2"]
        x2_ready = yield from transposed(x2, x2_t, x2_in, free.get("x2_t"), x_sum)
        free["x2_pe"] = pe.so_far()
        for t in range(TT):
            with_bo = tt(pool, x2_bo[:, t, :], x2[:, t, :], bo_s, ALU.add, x2_in, free.get("y_c"))
        free["x2_pool"] = with_bo
        bank, name, bank_free = g_take()
        for t in range(TT):
            for k in range(KT):
                last = mm(bank[0:1, 0:HF], x_sum[:, t, k:k + 1], wr_s[:, k, :], t + k == 0, t + k == KT, x2_ready, bank_free, mark=t + k == KT)
        yield
        free["x_sum"] = last
        free[name] = m = stt(r_lg, bank[0:1, 0:HF], 1.0 / T, br_s, ALU.mult, ALU.add, last)
        yield
        m = dve.do(lambda s: nc.vector.max(r_top, r_lg), m, apart=True)
        m = ts(dve, r_s[:, 0:1], r_top[:, 0:1], -1.0, None, ALU.mult, None, m)
        m = A(r_e, r_lg, ACT.Exp, m, bias=r_s[:, 0:1], accum_out=r_s[:, 1:2])
        yield
        m = dve.do(lambda s: nc.vector.reciprocal(r_s[:, 2:3], r_s[:, 1:2]), m)
        m = ts(dve, r_dist, r_e, r_s[:, 2:3], None, ALU.mult, None, m)
        m = dve.do(lambda s: nc.vector.max(r_dtop, r_dist), m, apart=True)
        picked = dve.do(lambda s: nc.vector.max_index(r_idx, r_dtop, r_dist), m, apart=True)
        m = ts(dve, r_s[:, 3:4], r_dtop[:, 0:1], -1.0, None, ALU.mult, None, m)
        A(r_eg, r_dtop[:, 0:KF], ACT.Exp, m, bias=r_s[:, 3:4], accum_out=r_s[:, 4:5])
        m = A(r_s[:, 5:6], r_dtop[:, 0:1], ACT.Exp, scale=-1.0)
        for k in range(KF):
            half = slice(DF * (k % 2), DF * (k % 2) + DF)

            def gather(s, k=k, half=half):
                h = nc.gpsimd.value_load(r_idx[0:1, k:k + 1], min_val=0, max_val=HF - 1)
                return nc.gpsimd.tensor_copy(b_sel[half, :, k // 2:k // 2 + 1], bias_col[half, :, bass.ds(h, 1)])
            b_picked = pool.do(gather, picked, *free.get("b_sel", ()), pool.so_far(), apart=True)
        pool.wait(b_picked)
        columns = []

        def fetch(s, j, k):
            if j == 0:
                columns.append(nc.sync.value_load(r_idx[0:1, k:k + 1], min_val=0, max_val=HF - 1) * DF)
            return nc.sync.dma_start(w_raw[j][:, :, k, :], col((wq, wk, wv)[j])[:, :, bass.ds(columns[-KF:][k] if j else columns[-1], DF)])
        w_in = []
        for j in range(3):
            for k in range(KF):
                m3 = sp.do(lambda s, j=j, k=k: fetch(s, j, k), picked, *free.get("w_raw", ()), sem=s_w[j], by=16, apart=True)
            w_in.append(m3)
        yield
        m = stt(r_s[:, 6:7], r_s[:, 5:6], float(HF - KF), r_s[:, 4:5], ALU.mult, ALU.add, m)
        m = dve.do(lambda s: nc.vector.reciprocal(r_s[:, 7:8], r_s[:, 6:7]), m)
        m = ts(dve, r_g[:, 0:KF], r_eg, r_s[:, 7:8], None, ALU.mult, None, m)
        m = stt(r_g[:, KF:], r_g[:, 0:KF], float(DF) ** -0.5, r_g[:, 0:KF], ALU.mult, ALU.mult, m)
        yield
        bank, name, bank_free = g_take()
        last = mm(bank[:, 0:2 * KF], ones[0:1, :], r_g, True, True, m, bank_free, mark=True)
        yield
        free[name] = g_ready = copy(dve, g_bc, bank[:, 0:2 * KF], last, free.get("g_bc"))
        yield
        w_ready = []
        for j in range(3):
            w_picked = split(part(w_sel, slice(None), slice(None), j), w_raw[j], None, w_in[j], free.get("w_sel"))
            w_ready.append(w_picked)
            yield
        for j, dst in enumerate((q_f, k_f)):
            bank, name, bank_free = g_take()
            for m in range(2):
                for k in range(KT):
                    w = [h.rearrange("p h d -> p (h d)") for h in part(w_sel, slice(None), k, j, slice(2 * m, 2 * m + 2))]
                    last = mm3(bank[:, m * T:(m + 1) * T], w, part(x2_t, slice(None), k), k == 0, k == KT - 1, w_ready[j], bank_free, mark=k == KT - 1)
                yield
            for m in range(2):
                qk_ready = ts(dve, dst[:, m, :], bank[:, m * T:(m + 1) * T], b_sel[:, j, m:m + 1], None, ALU.add, None, last, b_picked, free.get("qk_f"))
            free[name] = qk_ready
            yield
        for half in range(2):
            rows = slice(DF * half, DF * (half + 1))
            gate_row = g_bc[rows, half:KF:2]
            gated = tt(pool, b_v[rows, :], b_sel[rows, 2, :], gate_row, ALU.mult, b_picked, g_ready, free.get("b_v"), pool.so_far())
        pool.wait(gated)
        free["b_sel"] = (qk_ready, gated)
        bank, name, bank_free = g_take()
        for t in range(TT):
            for k in range(KT):
                w = [h.rearrange("p h d -> p (h d)") for h in part(w_sel, slice(None), k, 2)]
                last = mm3(bank[:, t * T:(t + 1) * T], part(x2_t, slice(None), k, slice(t * P, (t + 1) * P)), w, k == 0, k == KT - 1, w_ready[2], bank_free, mark=k == KT - 1)
            yield
        v_ready = free[name] = copy(act, v_f, bank.rearrange("p (t n) -> p t n", t=TT), last, free.get("v_f"))
        free["w_sel"] = last
        projected = last
        yield

        def scores(k):
            rows = slice(DF * (k % 2), DF * (k % 2) + DF)
            bank, name, bank_free = g_take()
            for t in range(TT):
                last = mm(bank[:, t * T:(t + 1) * T], q_f[rows, k // 2, t * P:(t + 1) * P], k_f[rows, k // 2, :], True, True, qk_ready, bank_free, mark=t == TT - 1)
            free["qk_f"] = last
            yield
            m = red(f_max[:, k, :], bank.rearrange("p (t n) -> p t n", t=TT), ALU.max, last)
            m = ts(dve, f_bias[:, k, :], f_max[:, k, :], g_bc[:, KF + k:KF + k + 1], -1.0, ALU.mult, ALU.mult, m, g_ready, free.get(f"f_bias{k}"))
            for t in range(TT):
                e = A(p_f[k % 2][:, t, :], bank[:, t * T:(t + 1) * T], ACT.Exp, m, w_picked, free.get(f"p_f{k % 2}"), scale=g_bc[:, KF + k:KF + k + 1],
                      bias=f_bias[:, k, t:t + 1], accum_out=f_sum[:, k, t:t + 1])
            free[name] = free[f"f_bias{k}"] = e
            yield
            r = dve.do(lambda s: nc.vector.reciprocal(f_rec[:, k, :], f_sum[:, k, :]), e)
            for t in range(TT):
                n = ts(pool, p_f[k % 2][:, t, :], p_f[k % 2][:, t, :], f_rec[:, k, t:t + 1], g_bc[:, k:k + 1], ALU.mult, ALU.mult, r)
            free["g_bc"] = n
            return n

        def turn(k, ready):
            bank, name, bank_free = g_take()
            for kk in range(TT):
                for t in range(TT):
                    last = tr(bank[:, kk * T + t * P:kk * T + (t + 1) * P], p_f[k % 2][:, t, kk * P:(kk + 1) * P], eye, ready, bank_free, mark=t + kk == 2)
            free[f"p_f{k % 2}"] = last
            yield
            free[name] = copy(act if k % 2 else dve, pt_f[k % 2].rearrange("p k n -> p (k n)"), bank, last, free.get("pt_f"))
            return free[name]

        m = yield from scores(0)
        ready = [m]
        yield
        turned = []
        for k in range(KF):
            if k + 1 < KF:
                m = yield from scores(k + 1)
                ready.append(m)
                yield
            m = yield from turn(k, ready[k])
            turned.append(m)
            yield
            if k % 2:
                bank, name, bank_free = g_take()
                for kk in range(TT):
                    for j in range(2):
                        h = k - 1 + j
                        last = mm(bank[DF * j:DF * (j + 1), 0:T], v_f[:, kk, h * DF:(h + 1) * DF], pt_f[j][:, kk, :], kk == 0, kk == TT - 1,
                                  v_ready, *turned, bank_free, mark=kk + j == 2)
                free["pt_f"] = last
                yield
                hi, lo = part(att_f, slice(None), k // 2)
                m = A(hi, bank[:, 0:T], ACT.Identity, last, projected, gated, bias=b_v[:, k // 2:k // 2 + 1])
                attended = free[name] = free["b_v"] = stt(lo, bank[:, 0:T], b_v[:, k // 2:k // 2 + 1], hi.bitcast(F32), ALU.add, ALU.subtract, m)
                turned = []
                yield
        free["v_f"] = last
        ys = []
        for t in range(TT):
            bank, name, bank_free = g_take()
            for k in range(2):
                last = mm3(bank, part(att_f, slice(None), k, slice(t * P, (t + 1) * P)), part(wo_s, slice(None), k), k == 0, k == 1, attended, bank_free, mark=k == 1)
            yield
            free[name] = y = tt(dve, y_c[:, t, :], bank, x2_bo[:, t, :], ALU.add, last, with_bo)
            ys.append(y)
            yield
        free["x2_t"] = last
        mean, rstd = norm("c", y_c, ys)
        yield
        _, mv, rs, shift = ln["c"]
        m = stt(shift[:, :, 0], mv[:, :, 0], -1.0, rs[:, :, 0], ALU.mult, ALU.mult, mean, rstd, free.get("y_c"))
        for t in range(TT):
            e = A(y_out[:, t, :], y_c[:, t, :], ACT.Identity, m, w_picked, scale=rs[:, t, 0:1], bias=shift[:, t, 0:1])
        free["y_c"] = free["lnc"] = e
        free["y_out"] = act.do(lambda s: nc.scalar.dma_start(out[s - 2].rearrange("(t p) n -> p t n", p=P), y_out), e, sem=s_out, by=16)
        free["w_raw"] = (free["y_out"], free["p_f0"], free["p_f1"], free["pt_f"])
        yield

    def step(parts, last=False):
        running = {"a": lambda: part_a(last), "b": part_b, "c": part_c}
        running = {n: running[n]() for n in parts}
        idle[:], in_use[:] = range(RING), ()
        for n in ORDER:
            if n in running:
                next(running[n])
        for n in parts:
            assert next(running[n], "end") == "end", "ORDER leaves work undone"

    def end_part():
        for lane in lanes:
            lane.end_part()

    def next_step():
        for lane in lanes:
            lane.step += 1

    LEAD = 3
    TURNS = NB - LEAD - 1
    for parts in ("a", "ab", "abc"):
        step(parts)
        next_step()
    end_part()
    before = dict(counts)
    step("abc")
    end_part()
    per_turn = {s: n - before[s] for s, n in counts.items() if n > before[s]}

    def last_turn(m):
        if isinstance(m, tuple):
            return tuple(last_turn(n) for n in m)
        if m is None or m.count <= before.get(m.sem, 0):
            return m
        return Mark(m.sem, m.count + per_turn[m.sem] * (TURNS - 1))
    for marks in (free, done):
        for name, m in marks.items():
            marks[name] = last_turn(m)
    for s, n in per_turn.items():
        counts[s] += n * (TURNS - 1)
    for lane in lanes:
        lane.step += TURNS
    for parts in ("abc", "bc", "c"):
        step(parts, last=True)
        next_step()
    sp.wait(free["y_out"])
    end_part()

    def program(lane):
        def run(engine):
            lane.run(0, engine)
            with engine.Fori(0, TURNS) as turn:
                lane.run(1, engine, turn, per_turn)
            lane.run(2, engine)
        return run

    with nc.Block() as block:
        block.tensor(program(pe))
        block.scalar(program(act))
        block.vector(program(dve))
        block.gpsimd(program(pool))
        block.sync(program(sp))


INPUTS = ["x", "ctx_1024", "L0_attn_Wqkv", "L0_attn_Wout", "L0_xattn_igate_kernel", "L0_xattn_igate_bias",
          "L0_xattn_fgate_kernel", "L0_xattn_fgate_bias", "L0_xattn_rms_scale", "L0_ffn_Wq", "L0_ffn_bq", "L0_ffn_Wk",
          "L0_ffn_bk", "L0_ffn_Wv", "L0_ffn_bv", "L0_ffn_Wr", "L0_ffn_br", "L0_ffn_Wo", "L0_ffn_bo"]


def kernel(**inputs):
    import concourse.bacc as bacc
    from concourse.bass_utils import run_bass_kernel_spmd

    nc = bacc.Bacc("TRN2", target_bir_lowering=False, num_devices=1)
    arrays, args = {}, []
    for name in INPUTS:
        a = np.ascontiguousarray(inputs[name])
        arrays["in_" + name] = a
        args.append(nc.dram_tensor("in_" + name, a.shape, mybir.dt.from_np(a.dtype), kind="ExternalInput").ap())
    out = nc.dram_tensor("out", (NB, T, D), F32, kind="ExternalOutput").ap()
    build(nc, *args, out)
    r = run_bass_kernel_spmd(nc, [arrays], core_ids=[0])
    return r.results[0]["out"]
```
